# Optimizing a Trainium2 kernel written in Bass

```python
import numpy as np
import jax
import jax.numpy as jnp

def _softmax(x, axis=-1):
    return jax.nn.softmax(x, axis=axis)

def _gelu(x):
    return jax.nn.gelu(x, approximate=True)

def _silu(x):
    return jax.nn.silu(x)

def _sigmoid(x):
    return jax.nn.sigmoid(x)

def _layernorm(x, axis=-1, eps=1e-05):
    m = jnp.mean(x, axis=axis, keepdims=True)
    v = jnp.var(x, axis=axis, keepdims=True)
    return (x - m) / jnp.sqrt(v + eps)

def _scatter_add(tgt, idx, src, axis=0):
    return tgt.at[idx].add(src)

def _segment_sum(src, seg, n):
    return jax.ops.segment_sum(src, seg, n)
kernel_name = 'mk_sandwich_d1_jaxref_r4_e0faea'

def setup_inputs(seed: int=0):
    np.random.seed(seed)
    _w = jnp.asarray

    def _L0_attn_setup():
        import jax, jax.numpy as jnp
        import numpy as np
        import math
        B, L, D, MAXL = (4, 1024, 256, 4096)

        def _shift1(a):
            return jnp.concatenate([jnp.zeros_like(a[:, :1]), a[:, :-1]], axis=1)
        key = jax.random.key(seed)
        ks = jax.random.split(key, 12)
        s = 0.02

        def w(k, shape):
            return jax.random.normal(k, shape, jnp.float32) * s
        return {'x': jax.random.normal(ks[0], (B, L, D), jnp.float32), 'pos_phases': jax.random.normal(ks[1], (MAXL, D), jnp.float32) * math.pi, 'Wpv': w(ks[2], (D, D)), 'bpv': jnp.zeros((D,), jnp.float32), 'Wk': w(ks[3], (D, D)), 'bk': jnp.zeros((D,), jnp.float32), 'Wkv': w(ks[4], (D, D)), 'bkv': jnp.zeros((D,), jnp.float32), 'Wg1': w(ks[5], (2 * D, D)), 'bg1': jnp.zeros((D,), jnp.float32), 'Wg2': w(ks[6], (D, 1)), 'bg2': jnp.zeros((1,), jnp.float32), 'Wb1': w(ks[7], (D, D // 2)), 'bb1': jnp.zeros((D // 2,), jnp.float32), 'Wb2': w(ks[8], (D // 2, 2)), 'bb2': jnp.zeros((2,), jnp.float32), 'ln_g': jnp.ones((D,), jnp.float32), 'ln_b': jnp.zeros((D,), jnp.float32), 'Wo': w(ks[9], (D, D)), 'bo': jnp.zeros((D,), jnp.float32)}
    _L0_attn_in = _L0_attn_setup()

    def _L0_ffn_setup():
        import jax, jax.numpy as jnp
        import numpy as np
        D_IN = 256
        D_OUT = 256
        D_QUERY = 64
        N_HEADS = 8
        N_EXPERTS = 16384
        N_SQRT = 64
        TOPK = 10
        DQ_HALF = D_QUERY // 2
        key = jax.random.key(seed)
        ks = jax.random.split(key, 7)
        B, S = (2, 256)
        x = jax.random.normal(ks[0], (B, S, D_IN), dtype=jnp.float32)
        Wq = jax.random.normal(ks[1], (D_IN, D_QUERY * N_HEADS), dtype=jnp.float32) / np.sqrt(D_IN)
        bq = jnp.zeros((D_QUERY * N_HEADS,), dtype=jnp.float32)
        K1 = jax.random.normal(ks[2], (N_SQRT, DQ_HALF), dtype=jnp.float32)
        K2 = jax.random.normal(ks[3], (N_SQRT, DQ_HALF), dtype=jnp.float32)
        W_up = jax.random.normal(ks[4], (N_EXPERTS, D_OUT), dtype=jnp.float32)
        W_down = jax.random.normal(ks[5], (N_EXPERTS, D_IN), dtype=jnp.float32)
        return {'x': x, 'Wq': Wq, 'bq': bq, 'K1': K1, 'K2': K2, 'W_up': W_up, 'W_down': W_down}
    _L0_ffn_in = _L0_ffn_setup()
    _d = {'L0_attn_x': _L0_attn_in['x'], 'L0_attn_pos_phases': _L0_attn_in['pos_phases'], 'L0_attn_Wpv': _L0_attn_in['Wpv'], 'L0_attn_bpv': _L0_attn_in['bpv'], 'L0_attn_Wk': _L0_attn_in['Wk'], 'L0_attn_bk': _L0_attn_in['bk'], 'L0_attn_Wkv': _L0_attn_in['Wkv'], 'L0_attn_bkv': _L0_attn_in['bkv'], 'L0_attn_Wg1': _L0_attn_in['Wg1'], 'L0_attn_bg1': _L0_attn_in['bg1'], 'L0_attn_Wg2': _L0_attn_in['Wg2'], 'L0_attn_bg2': _L0_attn_in['bg2'], 'L0_attn_Wb1': _L0_attn_in['Wb1'], 'L0_attn_bb1': _L0_attn_in['bb1'], 'L0_attn_Wb2': _L0_attn_in['Wb2'], 'L0_attn_bb2': _L0_attn_in['bb2'], 'L0_attn_ln_g': _L0_attn_in['ln_g'], 'L0_attn_ln_b': _L0_attn_in['ln_b'], 'L0_attn_Wo': _L0_attn_in['Wo'], 'L0_attn_bo': _L0_attn_in['bo'], 'L0_ffn_Wq': _L0_ffn_in['Wq'], 'L0_ffn_bq': _L0_ffn_in['bq'], 'L0_ffn_K1': _L0_ffn_in['K1'], 'L0_ffn_K2': _L0_ffn_in['K2'], 'L0_ffn_W_up': _L0_ffn_in['W_up'], 'L0_ffn_W_down': _L0_ffn_in['W_down']}
    _x0 = _d['L0_attn_x']
    _d['L0_attn_x'] = jax.random.normal(jax.random.fold_in(jax.random.key(seed), 1), (2, 4096, 256), dtype=_x0.dtype)
    del _x0
    return _d

def reference(L0_attn_x, L0_attn_pos_phases, L0_attn_Wpv, L0_attn_bpv, L0_attn_Wk, L0_attn_bk, L0_attn_Wkv, L0_attn_bkv, L0_attn_Wg1, L0_attn_bg1, L0_attn_Wg2, L0_attn_bg2, L0_attn_Wb1, L0_attn_bb1, L0_attn_Wb2, L0_attn_bb2, L0_attn_ln_g, L0_attn_ln_b, L0_attn_Wo, L0_attn_bo, L0_ffn_Wq, L0_ffn_bq, L0_ffn_K1, L0_ffn_K2, L0_ffn_W_up, L0_ffn_W_down):

    def _L0_attn_ref(x, pos_phases, Wpv, bpv, Wk, bk, Wkv, bkv, Wg1, bg1, Wg2, bg2, Wb1, bb1, Wb2, bb2, ln_g, ln_b, Wo, bo):
        import jax, jax.numpy as jnp
        import numpy as np
        import math
        B, L, D, MAXL = (4, 1024, 256, 4096)

        def _shift1(a):
            return jnp.concatenate([jnp.zeros_like(a[:, :1]), a[:, :-1]], axis=1)
        Bq, Lq, Dq = x.shape
        sqrtD = jnp.sqrt(jnp.float32(Dq))
        pp = pos_phases[:Lq]
        pos_cos, pos_sin = (jnp.cos(pp), jnp.sin(pp))
        pos_values = x @ Wpv + bpv
        pos_mem_cos = jnp.cumsum(pos_cos * pos_values, axis=1)
        pos_mem_sin = jnp.cumsum(pos_sin * pos_values, axis=1)
        pos_ret = (pos_cos * pos_mem_cos + pos_sin * pos_mem_sin) / sqrtD
        key_ph = jnp.tanh(x @ Wk + bk) * jnp.pi
        key_cos, key_sin = (jnp.cos(key_ph), jnp.sin(key_ph))
        kv_values = x @ Wkv + bkv
        x_shifted = _shift1(x)
        gate_in = jnp.concatenate([x, x_shifted], axis=-1)
        gh = jax.nn.gelu(gate_in @ Wg1 + bg1, approximate=False)
        value_gates = jax.nn.sigmoid(gh @ Wg2 + bg2)
        kc_s = _shift1(key_cos)
        ks_s = _shift1(key_sin)
        kv_mem_cos = jnp.cumsum(kc_s * kv_values * value_gates, axis=1)
        kv_mem_sin = jnp.cumsum(ks_s * kv_values * value_gates, axis=1)
        gate_cumsum = jnp.maximum(jnp.cumsum(value_gates, axis=1), 1.0)
        kv_ret = (key_cos * kv_mem_cos + key_sin * kv_mem_sin) / (jnp.sqrt(gate_cumsum) * sqrtD)
        bh = jax.nn.gelu(x @ Wb1 + bb1, approximate=False)
        bw = jax.nn.softmax(bh @ Wb2 + bb2, axis=-1)
        blended = bw[..., 0:1] * pos_ret + bw[..., 1:2] * kv_ret
        mu = jnp.mean(blended, axis=-1, keepdims=True)
        var = jnp.var(blended, axis=-1, keepdims=True)
        ln = (blended - mu) / jnp.sqrt(var + 1e-05) * ln_g + ln_b
        return x + ln @ Wo + bo

    def _L0_ffn_ref(x, Wq, bq, K1, K2, W_up, W_down):
        import jax, jax.numpy as jnp
        import numpy as np
        D_IN = 256
        D_OUT = 256
        D_QUERY = 64
        N_HEADS = 8
        N_EXPERTS = 16384
        N_SQRT = 64
        TOPK = 10
        DQ_HALF = D_QUERY // 2
        B, S, _ = x.shape
        q = (x @ Wq + bq).reshape(B, S, N_HEADS, D_QUERY)
        q1, q2 = (q[..., :DQ_HALF], q[..., DQ_HALF:])
        s1 = jnp.einsum('bshd,nd->bshn', q1, K1)
        s2 = jnp.einsum('bshd,nd->bshn', q2, K2)
        v1, i1 = jax.lax.top_k(s1, TOPK)
        v2, i2 = jax.lax.top_k(s2, TOPK)
        all_scores = (v1[..., :, None] + v2[..., None, :]).reshape(B, S, N_HEADS, TOPK * TOPK)
        all_indices = (i1[..., :, None] * N_SQRT + i2[..., None, :]).reshape(B, S, N_HEADS, TOPK * TOPK)
        vals, best = jax.lax.top_k(all_scores, TOPK)
        expert_idx = jnp.take_along_axis(all_indices, best, axis=-1)
        w_down = W_down[expert_idx]
        w_up = W_up[expert_idx]
        scores = jax.nn.softmax(vals, axis=-1)
        h = jnp.einsum('bsd,bshkd->bshk', x, w_down)
        h = jax.nn.gelu(h, approximate=False) * scores
        out = jnp.einsum('bshk,bshkd->bsd', h, w_up)
        return out
    x = L0_attn_x
    x = x + _layernorm(_L0_attn_ref(_layernorm(x, axis=-1), L0_attn_pos_phases, L0_attn_Wpv, L0_attn_bpv, L0_attn_Wk, L0_attn_bk, L0_attn_Wkv, L0_attn_bkv, L0_attn_Wg1, L0_attn_bg1, L0_attn_Wg2, L0_attn_bg2, L0_attn_Wb1, L0_attn_bb1, L0_attn_Wb2, L0_attn_bb2, L0_attn_ln_g, L0_attn_ln_b, L0_attn_Wo, L0_attn_bo), axis=-1)
    x = x + _layernorm(_L0_ffn_ref(_layernorm(x, axis=-1), L0_ffn_Wq, L0_ffn_bq, L0_ffn_K1, L0_ffn_K2, L0_ffn_W_up, L0_ffn_W_down), axis=-1)
    return x

_drawn_inputs = setup_inputs


def setup_inputs(seed=0):
    import zlib

    import numpy as np

    out = dict(_drawn_inputs(seed))
    spreads = {'L0_attn_bpv': (0.0, 0.1),
     'L0_attn_bk': (0.0, 0.8),
     'L0_attn_bkv': (0.0, 0.1),
     'L0_attn_bg1': (0.0, 2.0),
     'L0_attn_bb1': (0.0, 0.8),
     'L0_attn_bb2': (0.0, 0.544),
     'L0_attn_ln_g': (1.0, 0.2),
     'L0_attn_ln_b': (0.0, 0.269),
     'L0_attn_bo': (0.0, 0.1),
     'L0_ffn_bq': (0.0, 0.1)}
    factors = {'L0_attn_Wkv': 4.857,
     'L0_attn_Wg1': 8.0,
     'L0_attn_Wg2': 8.0,
     'L0_attn_Wb1': 8.0,
     'L0_attn_Wb2': 8.0}
    for name, (base, spread) in spreads.items():
        noise = np.random.default_rng([zlib.crc32(name.encode()), seed]).standard_normal(out[name].shape)
        drawn = base * np.exp(spread * noise) if base else spread * noise
        out[name] = jnp.asarray(drawn.astype(out[name].dtype))
    for name, factor in factors.items():
        out[name] = (out[name] * factor).astype(out[name].dtype)
    return out
```

```python
from contextlib import ExitStack

from concourse import mybir
from concourse.alu_op_type import AluOpType as ALU

F32, F16, BF16, U16 = mybir.dt.float32, mybir.dt.float16, mybir.dt.bfloat16, mybir.dt.uint16
ACT = mybir.ActivationFunctionType
AX = mybir.AxisListType


class Queue:

    def __init__(self, nc, ctx, tag):
        self.nc, self.ctx, self.tag = nc, ctx, tag
        self.items, self.sems, self.counts = [], {}, {}

    def _step(self, name, waits, make, by):
        if name not in self.sems:
            self.sems[name] = self.ctx.enter_context(self.nc.semaphore(f"{self.tag}_{name}"))
            self.counts[name] = 0
        self.counts[name] += by
        self.items.append(([w for w in waits if w is not None], make, self.sems[name], by))
        return self.sems[name], self.counts[name]

    def step(self, name, waits, make):
        return self._step(name, waits, make, 1)

    def dma(self, name, waits, make):
        return self._step(name, waits, make, 16)

    def last_wait(self, waits):
        self.items.append((waits, None, None, 0))

    def run(self, eng):
        passed = {}
        for waits, make, sem, by in self.items:
            for other, value in waits:
                if passed.get(id(other), 0) < value:
                    eng.wait_ge(other, value)
                    passed[id(other)] = value
            if make is not None:
                make().then_inc(sem, by)
        self.items = []


class Bank:

    def __init__(self, tensor):
        self.t, self.free = tensor, []


def in_blocks(nc, pe, act, dve, pool, sp):
    with nc.Block() as block:
        block.tensor(pe.run)
        block.scalar(act.run)
        block.vector(dve.run)
        block.gpsimd(pool.run)
        block.sync(sp.run)


P = 128
D = 256
KD = D // P
HEADS = 8
NSQ = 64
TOPK = 10
LISTS = 2 * HEADS
SLOTS = HEADS * TOPK
NQ, NR = P, NSQ * NSQ // P
C = 256
NT = C // P
GROUP = 512 // NR
EPS = 1e-5
GATE_SCALE = 1024.0
GONE = -3.0e38
PAIRS = [(0, 1, 10, 0), (1, 1, 5, 10), (2, 1, 3, 15), (3, 2, 2, 18), (5, 5, 1, 22)]
NPAIR = 27
LAG = 2


def experts_phase(nc, ctx, sems, chunks, x1_dram, out_dram, w, x1_ready=None):
    sb = lambda name, shape, dt: ctx.enter_context(nc.sbuf_tensor(name, shape, dt))
    ps = lambda name: Bank(ctx.enter_context(nc.psum_tensor(name, [P, 512], F32)))
    pe, act, dve, pool, sp = (Queue(nc, sems, t) for t in ("pe_b", "act_b", "dve_b", "pool_b", "sp_b"))
    T, V, S, G = nc.tensor, nc.vector, nc.scalar, nc.gpsimd

    ident = sb("b_ident", [P, P], F32)
    ident16 = sb("b_ident16", [P, P], F16)
    pair_no = sb("b_pair_no", [P, NPAIR * NT], F16)
    minus_half = sb("b_minus_half", [P, NT], F32)
    wq = sb("b_wq", [P, KD, HEADS * 64], F32)
    bq = sb("b_bq", [P, 4], F32)
    keys = sb("b_keys", [P, 256], F32)
    wdown = sb("b_wdown", [P, KD, NR, NQ], F32)
    wup = sb("b_wup", [P, 4, 2, D], F32)
    x1 = sb("b_x1", [P, NT, D], F32)
    x1t = sb("b_x1t", [P, NT, D], F32)
    xn = sb("b_xn", [P, NT, D], F32)
    xT = sb("b_xT", [P, 3, KD, C], F32)
    qT = sb("b_qT", [P, 4, C], F32)
    work = sb("b_work", [P, SLOTS * NPAIR * NT], F16)
    score = work[:, 0:NT * LISTS * NSQ * 2].bitcast(F32).rearrange("p (t l n) -> p t l n", t=NT, l=LISTS) \
        if 2 * NT * LISTS * NSQ <= SLOTS * NPAIR * NT else None
    val = sb("b_val", [P, NT, LISTS, 16], F32)
    idx = sb("b_idx", [P, NT, LISTS, 16], U16)
    id1 = sb("b_id1", [P, NT * HEADS, TOPK], F32)
    id2 = sb("b_id2", [P, NT * HEADS, TOPK], F32)
    cand = sb("b_cand", [P, NT * HEADS, NPAIR], F32)
    cid = sb("b_cid", [P, HEADS, NPAIR, NT], F16)
    top = sb("b_top", [P, NT * HEADS, 16], F32)
    pos = sb("b_pos", [P, NT * HEADS, 16], U16)
    posf = sb("b_posf", [P, SLOTS, NT], F16)
    gate = sb("b_gate", [P, NT, SLOTS], F32)
    gsum = sb("b_gsum", [P, NT * HEADS], F32)
    ghi = sb("b_ghi", [SLOTS, C], F16)
    glo = sb("b_glo", [SLOTS, C], F16)
    eid = sb("b_eid", [SLOTS, 4, C], U16)
    qid = sb("b_qid", [SLOTS, C], F16)
    rid = sb("b_rid", [SLOTS, C], F16)
    ohq = sb("b_ohq", [SLOTS, NQ, C], F16)
    ohr_hi = sb("b_ohr_hi", [SLOTS, NR, P], F16)
    ohr_lo = sb("b_ohr_lo", [SLOTS, NR, P], F16)
    gates = sb("b_gates", [P, NR, C], F32)
    hid = sb("b_hid", [P, 4, 2, C], F32)
    stat = sb("b_stat", [P, 2, NT, 6], F32)
    mv = sb("b_mv", [P, 2, NT, 2], F32)
    rstd = sb("b_rstd", [P, 2, NT], F32)
    y = sb("b_y", [P, NT, D], F32)
    sbank = [ps("b_ps_s0"), ps("b_ps_s1")]
    hbank = [ps("b_ps_h0"), ps("b_ps_h1")]
    abank = [ps("b_ps_a0"), ps("b_ps_a1")]
    mbank = [ps("b_ps_m0"), ps("b_ps_m1")]
    misc_turn = [0]

    def misc():
        misc_turn[0] += 1
        return mbank[misc_turn[0] % 2]

    ev = {}
    get = ev.get

    loads = {}
    for name, dst, src in (("ident", ident, w["ident"]), ("ident16", ident16, w["ident16"]),
                           ("pair_no", pair_no, w["pair_no"]), ("keys", keys, w["keys"]), ("bq", bq, w["bq"])):
        loads[name] = sp.dma("consts", [], lambda d=dst, s=src: nc.sync.dma_start(d[:, :], s))
    consts = loads["bq"]
    wq_in = sp.dma("wq", [], lambda: nc.sync.dma_start(wq[:, :, :], w["wq"].rearrange("(k p) n -> p k n", p=P)))
    wd_in = sp.dma("wdown", [], lambda: nc.sync.dma_start(wdown[:, :, :, :], w["wdown"].rearrange("(k p) r q -> p k r q", p=P)))
    half_set = pool.step("half", [], lambda: G.memset(minus_half[:, :], -0.5))

    x1_view = x1_dram.rearrange("(m t p) d -> m p t d", t=NT, p=P)
    out_view = out_dram.rearrange("(m t p) d -> m p t d", t=NT, p=P)

    def layernorm(which, m, src_of, src_ready, dst, dst_free):
        def stats():
            for t in range(NT):
                last = V.bn_stats(stat[:, which, t, :], src_of(t))
            return last
        a = dve.step(f"stats{which}", src_ready + [get((f"aggr{which}", m - 1))], stats)

        def aggr():
            for t in range(NT):
                last = V.bn_aggr(mv[:, which, t, :], stat[:, which, t, :])
            return last
        b = ev[(f"aggr{which}", m)] = dve.step(f"aggr{which}", [a, get((f"norm{which}", m - 1))], aggr)
        c = pool.step(f"eps{which}", [b, get((f"norm{which}", m - 1))],
                      lambda: G.tensor_scalar(rstd[:, which, :], mv[:, which, :, 1], EPS, None, ALU.add))
        d = pool.step(f"rstd{which}", [c, half_set],
                      lambda: G.tensor_tensor(rstd[:, which, :], rstd[:, which, :], minus_half[:, :], ALU.pow))

        def norm():
            for t in range(NT):
                last = V.tensor_scalar(dst[:, t, :], src_of(t), mv[:, which, t, 0:1], rstd[:, which, t:t + 1],
                                       ALU.subtract, ALU.mult)
            return last
        e = ev[(f"norm{which}", m)] = dve.step(f"norm{which}", [d] + dst_free, norm)
        return e

    def load_and_norm(m):
        a = sp.dma("x1", [get(("norm0", m - 1)), x1_ready],
                   lambda: nc.sync.dma_start(x1[:, :, :], x1_view[m]))
        layernorm(0, m, lambda t: x1[:, t, :], [a], xn, [get(("xT_pe", m - 1))])

    def scores(m):
        bank = misc()

        def tr():
            for k in range(KD):
                for t in range(NT):
                    last = T.transpose(bank.t[:, k * C + t * P:k * C + (t + 1) * P], xn[:, t, k * P:(k + 1) * P], ident[:, :])
            return last
        a = ev[("xT_pe", m)] = pe.step("xT", [ev[("norm0", m)], consts] + bank.free, tr)
        b = ev[("xT", m)] = act.step("xT", [a, get(("hid_pe", m - 3))],
                                     lambda: S.copy(xT[:, m % 3, :, :], bank.t[:, :].rearrange("p (k c) -> p k c", k=KD)))
        bank.free = [b]
        q_done = []
        for half in range(2):
            bank = misc()

            def proj(half=half, bank=bank):
                for j in range(2):
                    for k in range(KD):
                        n = 2 * half + j
                        last = T.matmul(bank.t[:, j * C:(j + 1) * C], wq[:, k, n * P:(n + 1) * P], xT[:, m % 3, k, :],
                                        start=k == 0, stop=k == KD - 1)
                return last
            c = pe.step("q", [b, wq_in] + bank.free, proj)

            def evac(half=half, bank=bank):
                for j in range(2):
                    n = 2 * half + j
                    last = S.activation(qT[:, n, :], bank.t[:, j * C:(j + 1) * C], ACT.Identity, bias=bq[:, n:n + 1])
                return last
            d = act.step("q", [c, consts, get(("score_pe", m - 1))], evac)
            bank.free = [d]
            q_done.append(d)
        for t in range(NT):
            for half in range(2):
                bank = misc()

                def sc(t=t, half=half, bank=bank):
                    for j in range(2):
                        last = T.matmul(bank.t[:, j * 256:(j + 1) * 256], qT[:, 2 * half + j, t * P:(t + 1) * P], keys[:, :],
                                        start=True, stop=True)
                    return last
                e = pe.step("score", [q_done[half], consts] + bank.free, sc)
                f = act.step("score", [e, get(("picks_pe", m - 1))],
                             lambda t=t, half=half, bank=bank: S.copy(
                                 score[:, t, 8 * half:8 * half + 8, :].rearrange("p l n -> p (l n)"), bank.t[:, :]))
                bank.free = [f]
            ev[("score", m, t)] = f
        ev[("score_pe", m)] = e

    def top_ten(name, lists, src, vals, ids, ready):
        def each(f):
            def run():
                for l in range(lists):
                    last = f(l)
                return last
            return run
        a = dve.step(name, ready, each(lambda l: V.max(vals(l)[:, 0:8], src(l))))
        b = dve.step(name, [a], each(lambda l: V.max_index(ids(l)[:, 0:8], vals(l)[:, 0:8], src(l))))
        c = dve.step(name, [b], each(lambda l: V.match_replace(src(l), vals(l)[:, 0:8], src(l), GONE)))
        d = dve.step(name, [c], each(lambda l: V.max(vals(l)[:, 8:16], src(l))))
        return dve.step(name, [d], each(lambda l: V.max_index(ids(l)[:, 8:16], vals(l)[:, 8:16], src(l))))

    def lists_top(m, t):
        ev[("lists", m, t)] = top_ten(f"lists{t}", LISTS, lambda l: score[:, t, l, :], lambda l: val[:, t, l, :],
                                      lambda l: idx[:, t, l, :],
                                      [ev[("score", m, t)], get(("cand", m - 1)), get(("ids_f", m - 1))])

    def pick(m):
        both = [ev[("lists", m, t)] for t in range(NT)]
        v = val[:, :, :, :].rearrange("p t (h s) k -> p (t h) s k", s=2)
        i = idx[:, :, :, :].rearrange("p t (h s) k -> p (t h) s k", s=2)
        TH = NT * HEADS

        def ids_f():
            V.tensor_scalar(id1[:, :, :], i[:, :, 0, 0:TOPK], float(NSQ), -2048.0, ALU.mult, ALU.add)
            return V.tensor_scalar(id2[:, :, :], i[:, :, 1, 0:TOPK], 0.0, None, ALU.add)
        a = ev[("ids_f", m)] = dve.step("ids_f", both + [get(("cid", m - 1))], ids_f)

        def make_cand():
            for a0, na, nb, off in PAIRS:
                dst = cand[:, :, off:off + na * nb].rearrange("p h (a b) -> p h a b", a=na)
                x = v[:, :, 0, a0:a0 + na].unsqueeze(3).to_broadcast([P, TH, na, nb])
                z = v[:, :, 1, 0:nb].unsqueeze(2).to_broadcast([P, TH, na, nb])
                last = G.tensor_tensor(dst, x, z, ALU.add)
            return last
        b = ev[("cand", m)] = pool.step("cand", both + [get(("pairs", m - 1))], make_cand)

        def make_cid():
            one = id1[:, :, :].rearrange("p (t h) k -> p t h k", t=NT)
            two = id2[:, :, :].rearrange("p (t h) k -> p t h k", t=NT)
            for t in range(NT):
                for a0, na, nb, off in PAIRS:
                    dst = cid[:, :, off:off + na * nb, t].rearrange("p h (a b) -> p h a b", a=na)
                    x = one[:, t, :, a0:a0 + na].unsqueeze(3).to_broadcast([P, HEADS, na, nb])
                    z = two[:, t, :, 0:nb].unsqueeze(2).to_broadcast([P, HEADS, na, nb])
                    last = G.tensor_tensor(dst, x, z, ALU.add)
            return last
        c = ev[("cid", m)] = pool.step("cid", [a, get(("picks", m - 1))], make_cid)
        d = ev[("pairs", m)] = top_ten("pairs", TH, lambda l: cand[:, l, :], lambda l: top[:, l, :],
                                       lambda l: pos[:, l, :], [b, get(("shift", m - 1)), get(("posf", m - 1))])

        g4 = gate[:, :, :].rearrange("p t (h k) -> p (t h) k", k=TOPK)
        e = ev[("shift", m)] = pool.step("shift", [d, get(("gate_pe", m - 1))], lambda: G.tensor_tensor(
            g4, top[:, :, 0:TOPK], top[:, :, 0:1].to_broadcast([P, TH, TOPK]), ALU.subtract))
        f = act.step("exp", [e], lambda: S.activation(g4, g4, ACT.Exp))
        g = dve.step("gsum", [f], lambda: V.tensor_reduce(gsum[:, :], g4, AX.X, ALU.add))
        h = dve.step("grecip", [g], lambda: V.reciprocal(gsum[:, :], gsum[:, :]))
        ev[("gate", m)] = pool.step("gate", [h], lambda: G.tensor_tensor(
            g4, g4, gsum[:, :].unsqueeze(2).to_broadcast([P, TH, TOPK]), ALU.mult))

        def make_posf():
            for t in range(NT):
                last = V.tensor_copy(posf[:, :, t].rearrange("p (h k) -> p h k", h=HEADS),
                                     pos[:, t * HEADS:(t + 1) * HEADS, 0:TOPK])
            return last
        j = ev[("posf", m)] = dve.step("posf", [d, get(("picks", m - 1))], make_posf)
        k = dve.step("mask", [j, consts, get(("picks_pe", m - 1))], lambda: V.tensor_tensor(
            work[:, :].rearrange("p (s c t) -> p s c t", s=SLOTS, c=NPAIR),
            posf[:, :, :].unsqueeze(2).to_broadcast([P, SLOTS, NPAIR, NT]),
            pair_no[:, :].rearrange("p (c t) -> p c t", t=NT).unsqueeze(1).to_broadcast([P, SLOTS, NPAIR, NT]), ALU.is_equal))
        w4 = work[:, :].rearrange("p (h k c) -> p h k c", h=HEADS, k=TOPK)
        ev[("picks", m)] = dve.step("picks", [k, c], lambda: V.tensor_tensor(
            w4, w4, cid[:, :, :, :].rearrange("p h c t -> p h (c t)").unsqueeze(2).to_broadcast([P, HEADS, TOPK, NPAIR * NT]),
            ALU.mult))

    def turn(m):
        bg, be = misc(), misc()

        def gates_pe():
            for t in range(NT):
                last = T.transpose(bg.t[0:SLOTS, t * P:(t + 1) * P], gate[:, t, :], ident[:, :])
            return last
        a = ev[("gate_pe", m)] = pe.step("gate", [ev[("gate", m)], consts] + bg.free, gates_pe)
        pk = work[:, :].rearrange("p (s c t) -> p s c t", s=SLOTS, c=NPAIR)

        def ids_pe():
            for t in range(NT):
                for c in range(NPAIR):
                    last = T.matmul(be.t[0:SLOTS, t * P:(t + 1) * P], pk[:, :, c, t], ident16[:, :],
                                    start=c == 0, stop=c == NPAIR - 1)
            return last
        b = ev[("picks_pe", m)] = pe.step("picks", [ev[("picks", m)]] + be.free, ids_pe)
        c = dve.step("ghi", [a, get(("ohr", m - 1, NT - 1))], lambda: V.tensor_scalar(
            ghi[:, :], bg.t[0:SLOTS, 0:C], GATE_SCALE, None, ALU.mult))
        d = dve.step("glo", [c], lambda: V.scalar_tensor_tensor(
            glo[:, :], bg.t[0:SLOTS, 0:C], GATE_SCALE, ghi[:, :], ALU.mult, ALU.subtract))
        bg.free = [d]
        e = dve.step("eid", [b], lambda: V.tensor_scalar(eid[:, 0, :], be.t[0:SLOTS, 0:C], 2048.0, None, ALU.add))
        be.free = [e]

        def fields():
            V.tensor_scalar(eid[:, 1, :], eid[:, 0, :], 6, None, ALU.logical_shift_right)
            V.tensor_scalar(eid[:, 2, :], eid[:, 0, :], 1, None, ALU.bitwise_and)
            return V.tensor_scalar(eid[:, 3, :], eid[:, 0, :], 1, NR - 1, ALU.logical_shift_right, ALU.bitwise_and)
        f = dve.step("fields", [e], fields)

        def numbers():
            V.scalar_tensor_tensor(qid[:, :], eid[:, 2, :], float(NSQ), eid[:, 1, :], ALU.mult, ALU.add)
            return V.tensor_copy(rid[:, :], eid[:, 3, :])
        ev[("ids", m)] = dve.step("numbers", [f, get(("ohq", m - 1))], numbers)
        ev[("gsplit", m)] = d

    def onehot_r(m, t):
        tok = slice(t * P, (t + 1) * P)
        free = [get(("gates_pe", m, t - 1) if t else ("gates_pe", m - 1, NT - 1))]

        def hot():
            for r in range(NR):
                last = V.tensor_scalar(ohr_lo[:, r, :], rid[:, tok], float(r), None, ALU.is_equal)
            return last
        a = dve.step("ohr", [ev[("ids", m)]] + free, hot)
        b = dve.step("ohr_hi", [a, ev[("gsplit", m)]], lambda: V.tensor_tensor(
            ohr_hi[:, :, :], ohr_lo[:, :, :], ghi[:, tok].unsqueeze(1).to_broadcast([SLOTS, NR, P]), ALU.mult))
        ev[("ohr", m, t)] = dve.step("ohr_lo", [b], lambda: V.tensor_tensor(
            ohr_lo[:, :, :], ohr_lo[:, :, :], glo[:, tok].unsqueeze(1).to_broadcast([SLOTS, NR, P]), ALU.mult))

    def onehot_q(m):
        def hot():
            for q in range(NQ):
                last = V.tensor_scalar(ohq[:, q, :], qid[:, :], float(q), None, ALU.is_equal)
            return last
        ev[("ohq", m)] = dve.step("ohq", [ev[("ids", m)], get(("gates_pe", m - 1, NT - 1))], hot)

    def gate_matrix(m, t):
        for g in range(P // GROUP):
            bank = sbank[g % 2]

            def mm(g=g, bank=bank):
                for n in range(GROUP):
                    tok = g * GROUP + n
                    dst = bank.t[:, n * NR:(n + 1) * NR]
                    T.matmul(dst, ohq[:, :, t * P + tok], ohr_hi[:, :, tok], start=True, stop=False)
                    last = T.matmul(dst, ohq[:, :, t * P + tok], ohr_lo[:, :, tok], start=False, stop=True)
                return last
            a = pe.step("gates", [ev[("ohq", m)], ev[("ohr", m, t)]] + bank.free, mm)
            tok0 = t * P + g * GROUP
            b = act.step("gates", [a, get(("mix", m - 1))], lambda bank=bank, tok0=tok0: S.mul(
                gates[:, :, tok0:tok0 + GROUP], bank.t[:, :].rearrange("p (n r) -> p r n", r=NR), 1.0 / GATE_SCALE))
            bank.free = [b]
        ev[("gates_pe", m, t)] = a
        ev[("gates", m)] = b

    def experts(m):
        mixed, wup_in = {}, {}
        for p in range(NR // 2 + LAG):
            if p < NR // 2:
                bank, slot = hbank[p % 2], p % 4
                n = m * (NR // 2) + p

                def down(p=p, bank=bank):
                    for j in range(2):
                        for k in range(KD):
                            last = T.matmul(bank.t[:, j * C:(j + 1) * C], wdown[:, k, 2 * p + j, :], xT[:, m % 3, k, :],
                                            start=k == 0, stop=k == KD - 1)
                    return last
                a = pe.step("down", [ev[("xT", m)], wd_in] + bank.free, down)
                b = act.step("gelu", [a, get(("up", n - 4))], lambda bank=bank, slot=slot: S.activation(
                    hid[:, slot, :, :], bank.t[:, :].rearrange("p (j c) -> p j c", j=2), ACT.Gelu))
                bank.free = [b]
                mixed[p] = pool.step("mix", [b, ev[("gates", m)]], lambda p=p, slot=slot: G.tensor_tensor(
                    hid[:, slot, :, :], hid[:, slot, :, :], gates[:, 2 * p:2 * p + 2, :], ALU.mult))
                wup_in[p] = sp.dma(f"wup{slot}", [get(("up", n - 4))], lambda p=p, slot=slot: nc.sync.dma_start(
                    wup[:, slot, :, :], w["wup"][:, 2 * p:2 * p + 2, :]))
            if p >= LAG:
                u = p - LAG

                def up(u=u):
                    for j in range(2):
                        for t in range(NT):
                            last = T.matmul(abank[t].t[:, 0:D], hid[:, u % 4, j, t * P:(t + 1) * P], wup[:, u % 4, j, :],
                                            start=u == 0 and j == 0, stop=u == NR // 2 - 1 and j == 1)
                    return last
                free = abank[0].free if u == 0 else []
                ev[("up", m * (NR // 2) + u)] = pe.step("up", [mixed[u], wup_in[u]] + free, up)
        ev[("mix", m)] = mixed[NR // 2 - 1]
        ev[("hid_pe", m)] = a
        ev[("acc", m)] = ev[("up", m * (NR // 2) + NR // 2 - 1)]

    def finish(m):
        a = sp.dma("x1t", [get(("res", m - 1)), x1_ready],
                   lambda: nc.sync.dma_start(x1t[:, :, :], x1_view[m]))
        e = layernorm(1, m, lambda t: abank[t].t[:, 0:D], [ev[("acc", m)]], y, [get(("out", m - 1))])
        for b in abank:
            b.free = [e]
        r = ev[("res", m)] = pool.step("res", [a, e], lambda: G.tensor_tensor(y[:, :, :], y[:, :, :], x1t[:, :, :], ALU.add))
        ev[("out", m)] = sp.dma("out", [r], lambda: nc.sync.dma_start(out_view[m], y[:, :, :]))

    def has(m):
        return 0 <= m < chunks

    for m in range(-3, chunks + 1):
        if has(m):
            gate_matrix(m, 0)
            onehot_r(m, 1)
        if has(m + 1):
            turn(m + 1)
        if has(m - 1):
            finish(m - 1)
        if has(m + 2):
            scores(m + 2)
            lists_top(m + 2, 0)
        if has(m):
            gate_matrix(m, 1)
        if has(m + 1):
            onehot_q(m + 1)
            onehot_r(m + 1, 0)
        if has(m + 2):
            lists_top(m + 2, 1)
            pick(m + 2)
        if has(m + 3):
            load_and_norm(m + 3)
        if has(m):
            experts(m)
    sp.last_wait([ev[("out", chunks - 1)]])
    return pe, act, dve, pool, sp


CA = 512
TA = CA // P
MAGIC = 12582912.0
TWO_PI = (6.28125, 0.0019350051879882812, 3.0199159819567534e-07)
PI = 3.1415925


def attention_phase(nc, ctx, sems, seqs, length, x_dram, x1_dram, w):
    sb = lambda name, shape, dt=F32: ctx.enter_context(nc.sbuf_tensor(name, shape, dt))
    ps = lambda name: Bank(ctx.enter_context(nc.psum_tensor(name, [P, 512], F32)))
    pe, act, dve, pool, sp = (Queue(nc, sems, t) for t in ("pe_a", "act_a", "dve_a", "pool_a", "sp_a"))
    T, V, S, G = nc.tensor, nc.vector, nc.scalar, nc.gpsimd
    chunks = seqs * length // CA

    ident, tri, last_row, ones = (sb(f"a_{n}", [P, P]) for n in ("ident", "tri", "last_row", "ones"))
    wproj = sb("a_wproj", [P, KD, 3 * D])
    wg1 = sb("a_wg1", [P, 2 * KD, D])
    wb1 = sb("a_wb1", [P, KD, P])
    wo = sb("a_wo", [P, KD, D])
    wg2 = sb("a_wg2", [P, KD])
    wb2 = sb("a_wb2", [P, 2])
    cols = sb("a_cols", [P, 7])
    head_b = sb("a_head_b", [P, 3])
    brow = sb("a_brow", [3, 5 * D])
    brest = sb("a_brest", [3, 5 * D])
    bpart = sb("a_bpart", [3, 3, 5 * D], BF16)
    bsum = sb("a_bsum", [3, 5 * D])
    bsplit = sb("a_bsplit", [3, 5 * D], BF16)
    row_mask = sb("a_row_mask", [3, 3])
    ones3 = sb("a_ones3", [3, P], BF16)
    minus_half = sb("a_minus_half", [P, TA])
    half_pi = sb("a_half_pi", [P, 1])
    ph = sb("a_ph", [P, TA * D])
    turns = sb("a_turns", [P, TA * D])
    cs = sb("a_cs", [P, 2, TA, 2, D])
    x = sb("a_x", [P, 4, TA, D])
    xn = sb("a_xn", [P, 4, TA, D])
    xT = sb("a_xT", [P, 4, KD, CA + 1])
    th = sb("a_th", [P, TA, D])
    tha = sb("a_tha", [P, TA, D])
    key = sb("a_key", [P, 2, TA, 2, D])
    keysh = sb("a_keysh", [P, 2, TA, 2, D])
    gh = sb("a_gh", [P, 3, CA])
    z = sb("a_z", [P, TA, 3])
    zmax = sb("a_zmax", [P, TA])
    den = sb("a_den", [P, 2, TA])
    gates = sb("a_gates", [P, 2, TA])
    gcum = sb("a_gcum", [P, 4, TA])
    fac = sb("a_fac", [P, 2, 2, TA])
    u = sb("a_u", [P, 2, 4 * D])
    carry = sb("a_carry", [P, seqs, 4 * D])
    prod = sb("a_prod", [P, 2, 2, 2, D])
    ret = sb("a_ret", [P, 2, 2, D])
    bl = sb("a_bl", [P, 2, TA, D])
    lnT = sb("a_lnT", [P, KD, CA])
    y = sb("a_y", [P, TA, D])
    stat = sb("a_stat", [P, 3, TA, 6])
    mv = sb("a_mv", [P, 3, TA, 2])
    rstd = sb("a_rstd", [P, 3, TA])
    tbank = [ps("a_ps_t0"), ps("a_ps_t1")]
    fbank = [ps("a_ps_f0"), ps("a_ps_f1")]
    pbank = [ps("a_ps_p0"), ps("a_ps_p1")]
    cbank = [ps("a_ps_c0"), ps("a_ps_c1")]
    turn_of = {"t": 0, "f": 0, "p": 0}

    def bank_of(kind):
        turn_of[kind] += 1
        return {"t": tbank, "f": fbank, "p": pbank}[kind][turn_of[kind] % 2]

    ev = {}
    get = ev.get

    loaded = None
    by_k = lambda a: a.rearrange("(k p) n -> p k n", p=P)
    for dst, src in ((ident[:, :], w["ident"]), (tri[:, :], w["tri"]), (last_row[:, :], w["last_row"]), (ones[:, :], w["ones"]),
                     (wproj[:, :, 0:D], by_k(w["wpv"])), (wproj[:, :, D:2 * D], by_k(w["wkv"])),
                     (wproj[:, :, 2 * D:3 * D], by_k(w["wk"])), (wg1[:, :, :], by_k(w["wg1"])), (wb1[:, :, :], by_k(w["wb1"])),
                     (wo[:, :, :], by_k(w["wo"])), (wg2[:, :], w["wg2"]), (wb2[:, :], w["wb2"]), (cols[:, :], w["cols"]),
                     (head_b[:, :], w["head_b"]), (brow[:, :], w["brow"]), (row_mask[:, :], w["row_mask"])):
        loaded = sp.dma("weights", [], lambda dst=dst, src=src: nc.sync.dma_start(dst, src))

    def set_constants():
        G.memset(minus_half[:, :], -0.5)
        G.memset(half_pi[:, :], PI / 2)
        G.memset(ones3[:, :], 1.0)
        for b in range(seqs):
            G.memset(keysh[0:1, b, 0, :, :], 0.0)
        return G.memset(carry[:, :, :], 0.0)
    constants = pool.step("constants", [], set_constants)

    s = dve.step("bias0", [loaded], lambda: V.tensor_copy(bpart[:, 0, :], brow[:, :]))
    s = dve.step("bias1", [s], lambda: V.tensor_tensor(brest[:, :], brow[:, :], bpart[:, 0, :], ALU.subtract))
    s = dve.step("bias2", [s], lambda: V.tensor_copy(bpart[:, 1, :], brest[:, :]))
    s = dve.step("bias3", [s], lambda: V.tensor_tensor(brest[:, :], brest[:, :], bpart[:, 1, :], ALU.subtract))
    s = dve.step("bias4", [s], lambda: V.tensor_copy(bpart[:, 2, :], brest[:, :]))
    s = dve.step("bias5", [s], lambda: V.tensor_scalar(bsum[:, :], bpart[:, 0, :], row_mask[:, 0:1], None, ALU.mult))
    s = dve.step("bias6", [s], lambda: V.scalar_tensor_tensor(bsum[:, :], bpart[:, 1, :], row_mask[:, 1:2], bsum[:, :],
                                                              ALU.mult, ALU.add))
    bias = dve.step("bias7", [s], lambda: V.scalar_tensor_tensor(bsplit[:, :], bpart[:, 2, :], row_mask[:, 2:3], bsum[:, :],
                                                                 ALU.mult, ALU.add))

    def where(n):
        j, b = divmod(n, seqs)
        rows = slice(b * length + j * CA, b * length + (j + 1) * CA)
        return j, b, rows

    def rows_of(dram, rows):
        return dram[rows, :].rearrange("(t p) d -> p t d", p=P)

    def layernorm(which, n, src, ready, dst, dst_free):
        def stats():
            for t in range(TA):
                last = V.bn_stats(stat[:, which, t, :], src(t))
            return last
        a = dve.step(f"stats{which}", ready + [get((f"aggr{which}", n - 1))], stats)

        def aggr():
            for t in range(TA):
                last = V.bn_aggr(mv[:, which, t, :], stat[:, which, t, :])
            return last
        b = ev[(f"aggr{which}", n)] = dve.step(f"aggr{which}", [a, get((f"norm{which}", n - 1))], aggr)
        c = pool.step(f"eps{which}", [b, get((f"norm{which}", n - 1))],
                      lambda: G.tensor_scalar(rstd[:, which, :], mv[:, which, :, 1], EPS, None, ALU.add))
        d = pool.step(f"rstd{which}", [c, constants],
                      lambda: G.tensor_tensor(rstd[:, which, :], rstd[:, which, :], minus_half[:, :], ALU.pow))

        def norm():
            for t in range(TA):
                last = V.tensor_scalar(dst(t), src(t), mv[:, which, t, 0:1], rstd[:, which, t:t + 1], ALU.subtract, ALU.mult)
            return last
        e = ev[(f"norm{which}", n)] = dve.step(f"norm{which}", [d] + dst_free, norm)
        return e

    def load(n):
        j, b, rows = where(n)
        a = ev[("x", n)] = sp.dma(f"x{n % 4}", [get(("x1", n - 4))],
                                  lambda: nc.sync.dma_start(x[:, n % 4, :, :], rows_of(x_dram, rows)))
        layernorm(0, n, lambda t: x[:, n % 4, t, :], [a], lambda t: xn[:, n % 4, t, :], [get(("y", n - 4))])

    def phases(j):
        slot = j % 2
        a = sp.dma("ph", [get(("cs", j - 1))], lambda: nc.sync.dma_start(
            ph[:, :].rearrange("p (t d) -> p t d", t=TA), rows_of(w["phases"], slice(j * CA, (j + 1) * CA))))
        b = dve.step("turns", [a, get(("cs", j - 1))], lambda: V.tensor_scalar(
            turns[:, :], ph[:, :], 0.15915494309189535, MAGIC, ALU.mult, ALU.add))
        b = dve.step("turns", [b], lambda: V.tensor_scalar(turns[:, :], turns[:, :], MAGIC, None, ALU.subtract))
        for part in TWO_PI:
            b = dve.step("reduce", [b], lambda part=part: V.scalar_tensor_tensor(
                ph[:, :], turns[:, :], -part, ph[:, :], ALU.mult, ALU.add))
        b = dve.step("clamp", [b], lambda: V.tensor_scalar(ph[:, :], ph[:, :], -PI, PI, ALU.max, ALU.min))
        c = act.step("ph_abs", [b], lambda: S.activation(turns[:, :], ph[:, :], ACT.Abs))
        four = lambda a: a.rearrange("p (t d) -> p t d", t=TA)

        def both():
            S.activation(cs[:, slot, :, 1, :], four(ph[:, :]), ACT.Sin)
            return S.activation(cs[:, slot, :, 0, :], four(turns[:, :]), ACT.Sin, bias=half_pi[:, :], scale=-1.0)
        ev[("cs", j)] = act.step("cs", [c, constants, get(("prod", (j - 2) * seqs + seqs - 1, TA - 1))], both)

    def turn_x(n):
        j, b, _ = where(n)
        slot = n % 4
        done = []
        for k in range(KD):
            bank = bank_of("t")

            def tr(k=k, bank=bank):
                for t in range(TA):
                    last = T.transpose(bank.t[:, t * P:(t + 1) * P], xn[:, slot, t, k * P:(k + 1) * P], ident[:, :])
                return last
            a = pe.step("xT", [ev[("norm0", n)], loaded] + bank.free, tr)
            c = act.step("xT", [a, get(("pv_pe", n - 4))], lambda k=k, bank=bank: S.copy(xT[:, slot, k, 1:CA + 1], bank.t[:, :]))
            bank.free = [c]
        if j:
            d = act.step("x_before", [c, ev[("xT", n - seqs)]],
                         lambda: S.copy(xT[:, slot, :, 0:1], xT[:, (n - seqs) % 4, :, CA:CA + 1]))
        else:
            d = pool.step("x_before", [], lambda: G.memset(xT[:, slot, :, 0:1], 0.0))
        ev[("xT", n)] = c
        ev[("x_before", n)] = d

    def keys(n):
        j, b, _ = where(n)
        slot = n % 2
        for half in range(2):
            bank = bank_of("f")

            def proj(half=half, bank=bank):
                T.matmul(bank.t[:, 0:D], ones3[:, :], bsplit[:, 2 * D:3 * D], start=True, stop=False, skip_group_check=True)
                T.matmul(bank.t[:, D:2 * D], ones3[:, :], bsplit[:, 2 * D:3 * D], start=False, stop=False, skip_group_check=True)
                for i in range(2):
                    t = 2 * half + i
                    for k in range(KD):
                        last = T.matmul(bank.t[:, i * D:(i + 1) * D], xT[:, n % 4, k, 1 + t * P:1 + (t + 1) * P],
                                        wproj[:, k, 2 * D:3 * D], start=False, stop=i == 1 and k == KD - 1, skip_group_check=True)
                return last
            a = pe.step("keys", [ev[("xT", n)], bias, constants] + bank.free, proj)
            c = act.step("tanh", [a, get(("key", n - 1))], lambda half=half, bank=bank: S.activation(
                th[:, 2 * half:2 * half + 2, :], bank.t[:, :].rearrange("p (t d) -> p t d", t=2), ACT.Tanh))
            bank.free = [c]
        ev[("tanh", n)] = c

    def key_waves(n):
        j, b, _ = where(n)
        slot = n % 2
        d = act.step("th_abs", [ev[("tanh", n)]], lambda: S.activation(tha[:, :, :], th[:, :, :], ACT.Abs))

        def both():
            S.activation(key[:, slot, :, 1, :], th[:, :, :], ACT.Sin, scale=PI)
            return S.activation(key[:, slot, :, 0, :], tha[:, :, :], ACT.Sin, bias=half_pi[:, :], scale=-PI)
        e = ev[("key", n)] = act.step("key", [d, constants, get(("prod", n - 2, TA - 1)), get(("keysh_in", n - 2)), get(("key_end", n - 2))], both)
        free = get(("u", n - 2, TA - 1))
        moves = [(keysh[1:113, slot, :, :, :], key[0:112, slot, :, :, :]),
                 (keysh[113:128, slot, :, :, :], key[112:127, slot, :, :, :]),
                 (keysh[0:1, slot, 1:TA, :, :], key[127:128, slot, 0:TA - 1, :, :])]
        for dst, src in moves:
            f = sp.dma(f"keysh{slot}", [e, free], lambda dst=dst, src=src: nc.sync.dma_start(dst, src))
        if j:
            f = sp.dma(f"keysh{slot}", [free, ev[("key_end", n - seqs)]],
                       lambda: nc.sync.dma_start(keysh[0:1, slot, 0, :, :], key_end[0:1, b, :, :]))
        ev[("key_end", n)] = sp.dma(f"key_end{b}", [e, f],
                                        lambda: nc.sync.dma_start(key_end[0:1, b, :, :], key[127:128, slot, TA - 1, :, :]))
        ev[("keysh_in", n)] = f

    key_end = sb("a_key_end", [1, seqs, 2, D])

    def gating(n):
        j, b, _ = where(n)
        slot = n % 4
        for m in range(3):
            bank = bank_of("f")

            def hidden(m=m, bank=bank):
                if m < 2:
                    parts = [(wg1[:, k, m * P:(m + 1) * P], xT[:, slot, k, 1:CA + 1]) for k in range(KD)] + \
                            [(wg1[:, KD + k, m * P:(m + 1) * P], xT[:, slot, k, 0:CA]) for k in range(KD)]
                else:
                    parts = [(wb1[:, k, :], xT[:, slot, k, 1:CA + 1]) for k in range(KD)]
                for i, (a, c) in enumerate(parts):
                    last = T.matmul(bank.t[:, :], a, c, start=i == 0, stop=i == len(parts) - 1)
                return last
            a = pe.step("hidden", [ev[("xT", n)], ev[("x_before", n)], loaded] + bank.free, hidden)
            c = act.step("hidden", [a, get(("logits", n - 1))], lambda m=m, bank=bank: S.activation(
                gh[:, m, :], bank.t[:, :], ACT.Gelu, bias=cols[:, m:m + 1]))
            bank.free = [c]
        bank = bank_of("f")

        def logits():
            for t in range(TA):
                tok = slice(t * P, (t + 1) * P)
                for m in range(2):
                    T.matmul(bank.t[:, 3 * t:3 * t + 1], gh[:, m, tok], wg2[:, m:m + 1], start=m == 0, stop=m == 1)
                last = T.matmul(bank.t[:, 3 * t + 1:3 * t + 3], gh[:, 2, tok], wb2[:, :], start=True, stop=True)
            return last
        a = ev[("logits", n)] = pe.step("logits", [c] + bank.free, logits)
        s = dve.step("z", [a, get(("fac", n - 1))], lambda: V.tensor_tensor(
            z[:, :, :], bank.t[:, 0:3 * TA].rearrange("p (t c) -> p t c", c=3),
            head_b[:, :].unsqueeze(1).to_broadcast([P, TA, 3]), ALU.add))
        bank.free = [s]
        s = dve.step("zmax", [s], lambda: V.tensor_tensor(zmax[:, :], z[:, :, 1], z[:, :, 2], ALU.max))

        def shift():
            V.tensor_scalar(z[:, :, 0], z[:, :, 0], -1.0, None, ALU.mult)
            return V.tensor_tensor(z[:, :, 1:3], z[:, :, 1:3], zmax[:, :].unsqueeze(2).to_broadcast([P, TA, 2]), ALU.subtract)
        s = dve.step("zshift", [s], shift)
        s = act.step("exp", [s], lambda: S.activation(z[:, :, :], z[:, :, :], ACT.Exp))

        def sums():
            V.tensor_scalar(den[:, 0, :], z[:, :, 0], 1.0, None, ALU.add)
            return V.tensor_tensor(den[:, 1, :], z[:, :, 1], z[:, :, 2], ALU.add)
        s = dve.step("den", [s], sums)
        s = dve.step("recip", [s], lambda: V.reciprocal(den[:, :, :], den[:, :, :]))

        s = dve.step("gate", [s, get(("u", n - 2, TA - 1)), get(("gcum_pe", n - 2))],
                     lambda: V.tensor_copy(gates[:, n % 2, :], den[:, 0, :]))
        gate = ev[("gate", n)] = s
        bank = bank_of("f")

        def gsum():
            g = gates[:, n % 2, :]
            last = T.matmul(bank.t[:, 0:TA], tri[:, :], g, start=True, stop=False)
            for t in range(TA - 1):
                for v in range(t + 1, TA):
                    last = T.matmul(bank.t[:, v:v + 1], ones[:, :], g[:, t:t + 1], start=False,
                                    stop=not j and t == TA - 2)
            if j:
                for t in range(TA):
                    last = T.matmul(bank.t[:, t:t + 1], last_row[:, :], gcum[:, (n - seqs) % 4, TA - 1:TA], start=False,
                                    stop=t == TA - 1)
            return last
        a = ev[("gcum_pe", n)] = pe.step("gcum", [gate, get(("gcum", n - seqs)) if j else None] + bank.free, gsum)
        s = ev[("gcum", n)] = dve.step("gcum", [a, get(("gcum_pe", n - 2))], lambda: V.tensor_copy(
            gcum[:, n % 4, :], bank.t[:, 0:TA]))
        bank.free = [s]
        s = dve.step("gmax", [s], lambda: V.tensor_scalar(zmax[:, :], gcum[:, n % 4, :], 1.0, None, ALU.max))
        s = pool.step("groot", [s, constants], lambda: G.tensor_tensor(zmax[:, :], zmax[:, :], minus_half[:, :], ALU.pow))
        s1 = dve.step("zscale", [s], lambda: V.scalar_tensor_tensor(
            z[:, :, 1:3], z[:, :, 1:3], 1.0 / 16, den[:, 1, :].unsqueeze(2).to_broadcast([P, TA, 2]), ALU.mult, ALU.mult))

        def factors():
            V.tensor_copy(fac[:, n % 2, 0, :], z[:, :, 1])
            return V.tensor_tensor(fac[:, n % 2, 1, :], z[:, :, 2], zmax[:, :], ALU.mult)
        ev[("fac", n)] = dve.step("fac", [s1, get(("blend", n - 2, TA - 1))], factors)

    def values(n, t):
        j, b, _ = where(n)
        bank = bank_of("p")

        def proj():
            T.matmul(bank.t[:, :], ones3[:, :], bsplit[:, 0:2 * D], start=True, stop=False)
            for k in range(KD):
                last = T.matmul(bank.t[:, :], xT[:, n % 4, k, 1 + t * P:1 + (t + 1) * P], wproj[:, k, 0:2 * D],
                                start=False, stop=k == KD - 1)
            return last
        a = ev[("pv_pe", n)] = pe.step("values", [ev[("xT", n)], bias, constants] + bank.free, proj)
        i = (n * TA + t) % 2
        twice = lambda v: v.unsqueeze(1).to_broadcast([P, 2, D])

        def terms():
            V.tensor_tensor(u[:, i, 0:2 * D].rearrange("p (s d) -> p s d", s=2), cs[:, j % 2, t, :, :],
                            twice(bank.t[:, 0:D]), ALU.mult)
            return V.scalar_tensor_tensor(u[:, i, 2 * D:4 * D].rearrange("p (s d) -> p s d", s=2), twice(bank.t[:, D:2 * D]),
                                          gates[:, n % 2, t:t + 1], keysh[:, n % 2, t, :, :], ALU.mult, ALU.mult)
        c = ev[("u", n, t)] = dve.step("u", [a, ev[("cs", j)], ev[("gate", n)], ev[("keysh_in", n)],
                                             get(("sum_pe", n * TA + t - 2))], terms)
        bank.free = [c]

    def sums(n, t):
        j, b, _ = where(n)
        i = (n * TA + t) % 2
        first = j == 0 and t == 0

        def cum():
            for h in range(2):
                last = T.matmul(cbank[h].t[:, :], tri[:, :], u[:, i, h * 512:(h + 1) * 512], start=True, stop=first)
            if not first:
                for h in range(2):
                    last = T.matmul(cbank[h].t[:, :], last_row[:, :], carry[:, b, h * 512:(h + 1) * 512], start=False, stop=True)
            return last
        a = ev[("sum_pe", n * TA + t)] = pe.step("sums", [ev[("u", n, t)], loaded, ev.get(("carry", b)), constants] + cbank[0].free, cum)

        def keep():
            for h in range(2):
                last = S.copy(carry[96:128, b, h * 512:(h + 1) * 512], cbank[h].t[96:128, :])
            return last
        c = ev[("carry", b)] = act.step("carry", [a], keep)

        def back():
            V.tensor_tensor(prod[:, i, 0, :, :], cbank[0].t[:, :].rearrange("p (s d) -> p s d", s=2), cs[:, j % 2, t, :, :], ALU.mult)
            return V.tensor_tensor(prod[:, i, 1, :, :], cbank[1].t[:, :].rearrange("p (s d) -> p s d", s=2),
                                   key[:, n % 2, t, :, :], ALU.mult)
        d = ev[("prod", n, t)] = dve.step("prod", [c, get(("ret", n * TA + t - 2))], back)
        for bank in cbank:
            bank.free = [d]
        e = ev[("ret", n * TA + t)] = pool.step("ret", [d, get(("blend", n * TA + t - 2))], lambda: G.tensor_tensor(
            ret[:, i, :, :], prod[:, i, :, 0, :], prod[:, i, :, 1, :], ALU.add))
        f = pool.step("ret_pos", [e, ev[("fac", n)]], lambda: G.tensor_scalar(
            ret[:, i, 0, :], ret[:, i, 0, :], fac[:, n % 2, 0, t:t + 1], None, ALU.mult))
        g = dve.step("blend", [f, get(("norm1", n - 2))], lambda: V.scalar_tensor_tensor(
            bl[:, n % 2, t, :], ret[:, i, 1, :], fac[:, n % 2, 1, t:t + 1], ret[:, i, 0, :], ALU.mult, ALU.add))
        ev[("blend", n, t)] = ev[("blend", n * TA + t)] = g

    def blend_norm(n):
        layernorm(1, n, lambda t: bl[:, n % 2, t, :], [ev[("blend", n, TA - 1)]], lambda t: bl[:, n % 2, t, :],
                  [])

    def output(n):
        j, b, rows = where(n)
        for k in range(KD):
            bank = bank_of("t")

            def tr(k=k, bank=bank):
                for t in range(TA):
                    last = T.transpose(bank.t[:, t * P:(t + 1) * P], bl[:, n % 2, t, k * P:(k + 1) * P], ident[:, :])
                return last
            a = ev[("lnT_pe", n)] = pe.step("lnT", [ev[("norm1", n)]] + bank.free, tr)
            c = act.step("lnT", [a, get(("wo_pe", n - 1)), loaded], lambda k=k, bank=bank: S.activation(
                lnT[:, k, :], bank.t[:, :], ACT.Identity, bias=cols[:, 5 + k:6 + k], scale=cols[:, 3 + k:4 + k]))
            bank.free = [c]
        ys = []
        for half in range(2):
            bank = bank_of("t")

            def proj(half=half, bank=bank):
                T.matmul(bank.t[:, :], ones3[:, :], bsplit[:, 3 * D:5 * D], start=True, stop=False, skip_group_check=True)
                for i in range(2):
                    t = 2 * half + i
                    for k in range(KD):
                        last = T.matmul(bank.t[:, i * D:(i + 1) * D], lnT[:, k, t * P:(t + 1) * P], wo[:, k, :],
                                        start=False, stop=i == 1 and k == KD - 1, skip_group_check=True)
                return last
            a = pe.step("wo", [c, bias] + bank.free, proj)
            d = dve.step("y", [a, get(("x1_out", n - 1))], lambda half=half, bank=bank: V.tensor_tensor(
                y[:, 2 * half:2 * half + 2, :], bank.t[:, :].rearrange("p (t d) -> p t d", t=2),
                xn[:, n % 4, 2 * half:2 * half + 2, :], ALU.add))
            bank.free = [d]
        ev[("wo_pe", n)] = a
        ev[("y", n)] = d
        e = layernorm(2, n, lambda t: y[:, t, :], [d], lambda t: y[:, t, :], [])
        f = ev[("x1", n)] = pool.step("x1", [e, ev[("x", n)]], lambda: G.tensor_tensor(
            y[:, :, :], y[:, :, :], x[:, n % 4, :, :], ALU.add))
        ev[("x1_out", n)] = sp.dma("x1", [f], lambda: nc.sync.dma_start(rows_of(x1_dram, rows), y[:, :, :]))

    def has(n):
        return 0 <= n < chunks

    for n in range(-2, chunks + 1):
        if has(n):
            values(n, 0)
        if has(n - 1):
            blend_norm(n - 1)
        if has(n + 2):
            load(n + 2)
            if (n + 2) % seqs == 0:
                phases((n + 2) // seqs)
        if has(n + 1):
            turn_x(n + 1)
        if has(n):
            values(n, 1)
            sums(n, 0)
        if has(n + 1):
            keys(n + 1)
        if has(n):
            values(n, 2)
            sums(n, 1)
        if has(n + 1):
            gating(n + 1)
        if has(n):
            values(n, 3)
            sums(n, 2)
        if has(n + 1):
            key_waves(n + 1)
        if has(n - 1):
            output(n - 1)
        if has(n):
            sums(n, 3)
    sp.last_wait([ev[("x1_out", chunks - 1)]])
    return (pe, act, dve, pool, sp), ev[("x1_out", chunks - 1)]


def build(nc, x, phases, wpv, wkv, wk, wg1, wg2, wb1, wb2, wo, cols, head_b, brow, row_mask, ident, tri, last_row, ones,
          ident16, wq, bq, keys, wdown, wup, pair_no, out, seqs, length):
    x1 = nc.dram_tensor("x1_between", [seqs * length, D], F32, kind="Internal").ap()
    with ExitStack() as sems:
        with ExitStack() as memory:
            queues, x1_written = attention_phase(
                nc, memory, sems, seqs, length, x, x1,
                dict(phases=phases, wpv=wpv, wkv=wkv, wk=wk, wg1=wg1, wg2=wg2, wb1=wb1, wb2=wb2, wo=wo, cols=cols, head_b=head_b,
                     brow=brow, row_mask=row_mask, ident=ident, tri=tri, last_row=last_row, ones=ones))
            in_blocks(nc, *queues)
        with ExitStack() as memory:
            queues = experts_phase(
                nc, memory, sems, seqs * length // C, x1, out,
                dict(ident=ident, ident16=ident16, pair_no=pair_no, keys=keys, bq=bq, wq=wq, wdown=wdown, wup=wup), x1_written)
            in_blocks(nc, *queues)


def kernel(**inputs):
    import numpy as np
    import concourse.bacc as bacc
    from concourse.bass_utils import run_bass_kernel_spmd

    a = {k.removeprefix("L0_"): np.asarray(v) for k, v in inputs.items()}
    x = a["attn_x"]
    seqs, length, width = x.shape
    by_feature = lambda v: v.reshape(-1, P).T
    in_rows = lambda v, n: np.tile(v, (n, 1))

    def experts_by_qr(table):
        return table[:NSQ * NSQ].reshape(NSQ, NR, 2, width)

    k1, k2 = a["ffn_K1"], a["ffn_K2"]
    half = k1.shape[1]
    keys = np.zeros((P, 4 * NSQ), k1.dtype)
    for i, k in enumerate((k1, k2, k1, k2)):
        keys[i * half:(i + 1) * half, i * NSQ:(i + 1) * NSQ] = k.T
    last_row = np.zeros((P, P), x.dtype)
    last_row[-1] = 1
    arrays = dict(
        x=x.reshape(-1, width), phases=a["attn_pos_phases"][:length],
        wpv=a["attn_Wpv"], wkv=a["attn_Wkv"], wk=a["attn_Wk"], wg1=a["attn_Wg1"], wg2=by_feature(a["attn_Wg2"]),
        wb1=a["attn_Wb1"], wb2=a["attn_Wb2"], wo=a["attn_Wo"],
        cols=np.concatenate([by_feature(a[n]) for n in ("attn_bg1", "attn_bb1", "attn_ln_g", "attn_ln_b")], 1),
        head_b=in_rows(np.concatenate([a["attn_bg2"], a["attn_bb2"]]), P),
        brow=in_rows(np.concatenate([a[n] for n in ("attn_bpv", "attn_bkv", "attn_bk", "attn_bo", "attn_bo")]), 3),
        row_mask=np.eye(3, dtype=x.dtype), ident=np.eye(P, dtype=x.dtype), tri=np.triu(np.ones((P, P), x.dtype)),
        last_row=last_row, ones=np.ones((P, P), x.dtype), ident16=np.eye(P, dtype=np.float16),
        wq=a["ffn_Wq"], bq=by_feature(a["ffn_bq"]), keys=keys,
        wdown=experts_by_qr(a["ffn_W_down"]).transpose(3, 1, 2, 0).reshape(width, NR, NQ),
        wup=experts_by_qr(a["ffn_W_up"]).transpose(2, 0, 1, 3).reshape(NQ, NR, width),
        pair_no=in_rows(np.repeat(np.arange(NPAIR), NT).astype(np.float16), P),
    )
    arrays = {k: np.ascontiguousarray(v) for k, v in arrays.items()}
    nc = bacc.Bacc("TRN2", target_bir_lowering=False, num_devices=1)
    args = {k: nc.dram_tensor(f"in_{k}", v.shape, mybir.dt.from_np(v.dtype), kind="ExternalInput").ap()
            for k, v in arrays.items()}
    out = nc.dram_tensor("out", [seqs * length, width], F32, kind="ExternalOutput").ap()
    build(nc, out=out, seqs=seqs, length=length, **args)
    got = run_bass_kernel_spmd(nc, [{f"in_{k}": v for k, v in arrays.items()}], core_ids=[0])
    return got.results[0]["out"].reshape(x.shape)
```

```python
from contextlib import ExitStack

from concourse import mybir
from concourse.alu_op_type import AluOpType as ALU

F32, F32R, F16, BF16, U16 = mybir.dt.float32, mybir.dt.float32r, mybir.dt.float16, mybir.dt.bfloat16, mybir.dt.uint16
ACT = mybir.ActivationFunctionType
AX = mybir.AxisListType


class Queue:

    def __init__(self, nc, ctx, tag):
        self.nc, self.ctx, self.tag = nc, ctx, tag
        self.items, self.sems, self.counts = [], {}, {}

    def _step(self, name, waits, make, by):
        if name not in self.sems:
            self.sems[name] = self.ctx.enter_context(self.nc.semaphore(f"{self.tag}_{name}"))
            self.counts[name] = 0
        self.counts[name] += by
        self.items.append(([w for w in waits if w is not None], make, self.sems[name], by))
        return self.sems[name], self.counts[name]

    def step(self, name, waits, make):
        return self._step(name, waits, make, 1)

    def dma(self, name, waits, make):
        return self._step(name, waits, make, 16)

    def last_wait(self, waits):
        self.items.append((waits, None, None, 0))

    def run(self, eng):
        passed = {}
        for waits, make, sem, by in self.items:
            for other, value in waits:
                if passed.get(id(other), 0) < value:
                    eng.wait_ge(other, value)
                    passed[id(other)] = value
            if make is not None:
                make().then_inc(sem, by)
        self.items = []


class Bank:

    def __init__(self, tensor):
        self.t, self.free = tensor, []


def in_blocks(nc, pe, act, dve, pool, sp):
    with nc.Block() as block:
        block.tensor(pe.run)
        block.scalar(act.run)
        block.vector(dve.run)
        block.gpsimd(pool.run)
        block.sync(sp.run)


P = 128
D = 256
KD = D // P
HEADS = 8
NSQ = 64
TOPK = 10
LISTS = 2 * HEADS
SLOTS = HEADS * TOPK
NQ, NR = P, NSQ * NSQ // P
C = 256
NT = C // P
GROUP = 512 // NR
EPS = 1e-5
GATE_SCALE = 1024.0
GONE = -3.0e38
PAIRS = [(0, 1, 10, 0), (1, 1, 5, 10), (2, 1, 3, 15), (3, 2, 2, 18), (5, 5, 1, 22)]
NPAIR = 27
LAG = 3
WD_SLOTS = 3


def experts_phase(nc, ctx, sems, chunks, x1_dram, out_dram, w, x1_ready=None):
    sb = lambda name, shape, dt: ctx.enter_context(nc.sbuf_tensor(name, shape, dt))
    ps = lambda name: Bank(ctx.enter_context(nc.psum_tensor(name, [P, 512], F32)))
    pe, act, dve, pool, sp = (Queue(nc, sems, t) for t in ("pe_b", "act_b", "dve_b", "pool_b", "sp_b"))
    T, V, S, G = nc.tensor, nc.vector, nc.scalar, nc.gpsimd

    ident = sb("b_ident", [P, P], F32)
    ident16 = sb("b_ident16", [P, P], F16)
    pair_no = sb("b_pair_no", [P, NPAIR * NT], F16)
    minus_half = sb("b_minus_half", [P, NT], F32)
    wq = sb("b_wq", [P, KD, HEADS * 64], F32)
    bq = sb("b_bq", [P, 4], F32)
    keys = sb("b_keys", [P, 256], F32)
    wdown = sb("b_wdown", [P, KD, NR, NQ], F32)
    wup = sb("b_wup", [P, 4, 2, D], F32)
    x1 = sb("b_x1", [P, NT, D], F32)
    x1t = sb("b_x1t", [P, NT, D], F32)
    xn = sb("b_xn", [P, NT, D], F32)
    xT_hi = sb("b_xT_hi", [P, 3, KD, C], F32R)
    xT_lo = sb("b_xT_lo", [P, 3, KD, C], F32R)
    wd_split = [sb(f"b_wd_split{i}", [P, 2, KD, 2, NQ], F32R) for i in range(WD_SLOTS)]
    work = sb("b_work", [P, SLOTS * NPAIR * NT], F16)
    score = work[:, 0:NT * LISTS * NSQ * 2].bitcast(F32).rearrange("p (t l n) -> p t l n", t=NT, l=LISTS) \
        if 2 * NT * LISTS * NSQ <= SLOTS * NPAIR * NT else None
    val = sb("b_val", [P, NT, LISTS, 16], F32)
    idx = sb("b_idx", [P, NT, LISTS, 16], U16)
    id1 = sb("b_id1", [P, NT, HEADS, TOPK], F32)
    id2 = sb("b_id2", [P, NT, HEADS, TOPK], F32)
    cand = sb("b_cand", [P, NT, HEADS, NPAIR], F32)
    cid = sb("b_cid", [P, HEADS, NPAIR, NT], F16)
    top = sb("b_top", [P, NT * HEADS, 16], F32)
    pos = sb("b_pos", [P, NT * HEADS, 16], U16)
    posf = sb("b_posf", [P, SLOTS, NT], F16)
    gate = sb("b_gate", [P, NT, SLOTS], F32)
    gsum = sb("b_gsum", [P, NT * HEADS], F32)
    ghi = sb("b_ghi", [SLOTS, 2, C], F16)
    glo = sb("b_glo", [SLOTS, 2, C], F16)
    gateT = sb("b_gateT", [SLOTS, C], F32)
    eid = sb("b_eid", [SLOTS, 4, C], U16)
    qid = sb("b_qid", [SLOTS, C], F16)
    rid = sb("b_rid", [SLOTS, 2, C], F16)
    ohq = sb("b_ohq", [SLOTS, NQ, C], F16)
    ohr_hi = sb("b_ohr_hi", [SLOTS, NR, P], F16)
    ohr_lo = sb("b_ohr_lo", [SLOTS, NR, P], F16)
    gates = sb("b_gates", [P, NR, C], F32)
    hid = sb("b_hid", [P, 4, 2, C], F32)
    qT = hid[:, 0:2, :, :].rearrange("p a b c -> p (a b) c")
    xT = hid[:, 3, :, :]
    stat = sb("b_stat", [P, 2, NT, 6], F32)
    mv = sb("b_mv", [P, 2, NT, 2], F32)
    rstd = sb("b_rstd", [P, 2, NT], F32)
    y = sb("b_y", [P, NT, D], F32)
    sbank = [ps("b_ps_s0"), ps("b_ps_s1")]
    hbank = [ps("b_ps_h0"), ps("b_ps_h1")]
    abank = [ps("b_ps_a0"), ps("b_ps_a1")]
    mbank = [ps("b_ps_m0"), ps("b_ps_m1")]
    misc_turn = [0]

    def misc():
        misc_turn[0] += 1
        return mbank[misc_turn[0] % 2]

    ev = {}
    get = ev.get

    loads = {}
    for name, dst, src in (("ident", ident, w["ident"]), ("ident16", ident16, w["ident16"]),
                           ("pair_no", pair_no, w["pair_no"]), ("keys", keys, w["keys"]), ("bq", bq, w["bq"])):
        loads[name] = sp.dma("consts", [], lambda d=dst, s=src: nc.sync.dma_start(d[:, :], s))
    consts = loads["bq"]
    wq_in = sp.dma("wq", [], lambda: nc.sync.dma_start(wq[:, :, :], w["wq"].rearrange("(k p) n -> p k n", p=P)))
    wd_in = sp.dma("wdown", [], lambda: nc.sync.dma_start(wdown[:, :, :, :], w["wdown"].rearrange("(k p) r q -> p k r q", p=P)))
    half_set = pool.step("half", [], lambda: G.memset(minus_half[:, :], -0.5))

    x1_view = x1_dram.rearrange("(m t p) d -> m p t d", t=NT, p=P)
    out_view = out_dram.rearrange("(m t p) d -> m p t d", t=NT, p=P)

    def moments(which, m, src_of, src_ready):
        def stats():
            for t in range(NT):
                last = V.bn_stats(stat[:, which, t, :], src_of(t))
            return last
        a = dve.step(f"stats{which}", src_ready + [get((f"aggr{which}", m - 1))], stats)

        def aggr():
            for t in range(NT):
                last = V.bn_aggr(mv[:, which, t, :], stat[:, which, t, :])
            return last
        b = ev[(f"aggr{which}", m)] = dve.step(f"aggr{which}", [a, get((f"norm{which}", m - 1))], aggr)

    def root(which, m):
        c = pool.step(f"eps{which}", [ev[(f"aggr{which}", m)], get((f"norm{which}", m - 1))],
                      lambda: G.tensor_scalar(rstd[:, which, :], mv[:, which, :, 1], EPS, None, ALU.add))
        ev[(f"rstd{which}", m)] = pool.step(f"rstd{which}", [c, half_set],
                      lambda: G.tensor_tensor(rstd[:, which, :], rstd[:, which, :], minus_half[:, :], ALU.pow))

    def normalise(which, m, src_of, dst, dst_free):
        def norm():
            for t in range(NT):
                last = V.tensor_scalar(dst[:, t, :], src_of(t), mv[:, which, t, 0:1], rstd[:, which, t:t + 1],
                                       ALU.subtract, ALU.mult)
            return last
        e = ev[(f"norm{which}", m)] = dve.step(f"norm{which}", [ev[(f"rstd{which}", m)]] + dst_free, norm)
        return e

    def load(m):
        a = sp.dma("x1", [get(("norm0", m - 1)), x1_ready],
                   lambda: nc.sync.dma_start(x1[:, :, :], x1_view[m]))
        moments(0, m, lambda t: x1[:, t, :], [a])

    def norm_in(m):
        normalise(0, m, lambda t: x1[:, t, :], xn, [get(("xT_pe", m - 1))])

    def turn_x(m):
        bank = misc()

        def tr():
            for k in range(KD):
                for t in range(NT):
                    last = T.transpose(bank.t[:, k * C + t * P:k * C + (t + 1) * P], xn[:, t, k * P:(k + 1) * P], ident[:, :])
            return last
        a = ev[("xT_pe", m)] = pe.step("xT", [ev[("norm0", m)], consts] + bank.free, tr)
        b = ev[("xT", m)] = act.step("xT", [a, get(("acc", m - 3))],
                                     lambda: S.copy(xT, bank.t[:, :].rearrange("p (k c) -> p k c", k=KD)))
        bank.free = [b]
        c = act.step("xT_hi", [b, get(("down_pe", m - 3))], lambda: S.copy(xT_hi[:, m % 3, :, :], xT))
        ev[("xT_split", m)] = pool.step("xT_lo", [c], lambda: G.tensor_tensor(
            xT_lo[:, m % 3, :, :], xT, xT_hi[:, m % 3, :, :].bitcast(F32), ALU.subtract))

    def scores(m):
        b = ev[("xT", m)]
        q_done = []
        for half in range(2):
            bank = hbank[half]

            def proj(half=half, bank=bank):
                for j in range(2):
                    for k in range(KD):
                        n = 2 * half + j
                        last = T.matmul(bank.t[:, j * C:(j + 1) * C], wq[:, k, n * P:(n + 1) * P], xT[:, k, :],
                                        start=k == 0, stop=k == KD - 1)
                return last
            c = pe.step("q", [b, wq_in] + bank.free, proj)

            def evac(half=half, bank=bank):
                for j in range(2):
                    n = 2 * half + j
                    last = S.activation(qT[:, n, :], bank.t[:, j * C:(j + 1) * C], ACT.Identity, bias=bq[:, n:n + 1])
                return last
            d = act.step("q", [c, consts, get(("score_pe", m - 1)), get(("acc", m - 3))], evac)
            bank.free = [d]
            q_done.append(d)
        for half in range(2):
            for t in range(NT):
                bank = (hbank if half else mbank)[t]

                def sc(t=t, half=half, bank=bank):
                    for j in range(2):
                        last = T.matmul(bank.t[:, j * 256:(j + 1) * 256], qT[:, 2 * half + j, t * P:(t + 1) * P], keys[:, :],
                                        start=True, stop=True)
                    return last
                e = pe.step("score", [q_done[half], consts] + bank.free, sc)
                f = act.step("score", [e, get(("picks_pe", m - 1))],
                             lambda t=t, half=half, bank=bank: S.copy(
                                 score[:, t, 8 * half:8 * half + 8, :].rearrange("p l n -> p (l n)"), bank.t[:, :]))
                bank.free = [f]
                ev[("score", m, t)] = f
        ev[("score_pe", m)] = e

    def top_ten(name, lists, src, vals, ids, ready):
        def each(f):
            def run():
                for l in range(lists):
                    last = f(l)
                return last
            return run
        a = dve.step(name, ready, each(lambda l: V.max(vals(l)[:, 0:8], src(l))))
        b = dve.step(name, [a], each(lambda l: V.max_index(ids(l)[:, 0:8], vals(l)[:, 0:8], src(l))))
        c = dve.step(name, [b], each(lambda l: V.match_replace(src(l), vals(l)[:, 0:8], src(l), GONE)))
        d = dve.step(name, [c], each(lambda l: V.max(vals(l)[:, 8:16], src(l))))
        return dve.step(name, [d], each(lambda l: V.max_index(ids(l)[:, 8:16], vals(l)[:, 8:16], src(l))))

    def lists_top(m, t):
        ev[("lists", m, t)] = top_ten(f"lists{t}", LISTS, lambda l: score[:, t, l, :], lambda l: val[:, t, l, :],
                                      lambda l: idx[:, t, l, :],
                                      [ev[("score", m, t)], get(("cand", m - 1, t)), get(("ids_f", m - 1, t))])

    def numbers(m, t):
        i = idx[:, t, :, :].rearrange("p (h s) k -> p h s k", s=2)

        def ids_f():
            V.tensor_scalar(id1[:, t, :, :], i[:, :, 0, 0:TOPK], float(NSQ), -2048.0, ALU.mult, ALU.add)
            return V.tensor_scalar(id2[:, t, :, :], i[:, :, 1, 0:TOPK], 0.0, None, ALU.add)
        ev[("ids_f", m)] = ev[("ids_f", m, t)] = dve.step("ids_f", [ev[("lists", m, t)], get(("cid", m - 1, t))], ids_f)

    pairing = [(pool, G)] + [(dve, V)] * (NT - 1)

    def pairs_of(eng, dst, one, two):
        for a0, na, nb, off in PAIRS:
            last = eng.tensor_tensor(dst[:, :, off:off + na * nb].rearrange("p h (a b) -> p h a b", a=na),
                                   one[:, :, a0:a0 + na].unsqueeze(3).to_broadcast([P, HEADS, na, nb]),
                                   two[:, :, 0:nb].unsqueeze(2).to_broadcast([P, HEADS, na, nb]), ALU.add)
        return last

    def pair_sums(m, t):
        v = val[:, t, :, :].rearrange("p (h s) k -> p h s k", s=2)
        ev[("cand", m)] = ev[("cand", m, t)] = pairing[t][0].step("cand", [ev[("lists", m, t)], get(("pairs", m - 1, t))], lambda: pairs_of(pairing[t][1],
            cand[:, t, :, :], v[:, :, 0, :], v[:, :, 1, :]))

    def pair_numbers(m, t):
        ev[("cid", m)] = ev[("cid", m, t)] = pairing[t][0].step("cid", [ev[("ids_f", m, t)], get(("picks", m - 1))], lambda: pairs_of(pairing[t][1],
            cid[:, :, :, t], id1[:, t, :, :], id2[:, t, :, :]))

    def pairs_top(m, t):
        ev[("pairs", m, t)] = top_ten(f"pairs{t}", HEADS, lambda l: cand[:, t, l, :], lambda l: top[:, t * HEADS + l, :],
                                      lambda l: pos[:, t * HEADS + l, :],
                                      [ev[("cand", m, t)], get(("shift", m - 1)), get(("posf", m - 1))])

    def pick(m):
        def make_posf():
            for t in range(NT):
                last = V.tensor_copy(posf[:, :, t].rearrange("p (h k) -> p h k", h=HEADS),
                                     pos[:, t * HEADS:(t + 1) * HEADS, 0:TOPK])
            return last
        j = ev[("posf", m)] = dve.step("posf", [ev[("pairs", m, NT - 1)], get(("picks", m - 1))], make_posf)
        k = dve.step("mask", [j, consts, get(("picks_pe", m - 1))], lambda: V.tensor_tensor(
            work[:, :].rearrange("p (s c t) -> p s c t", s=SLOTS, c=NPAIR),
            posf[:, :, :].unsqueeze(2).to_broadcast([P, SLOTS, NPAIR, NT]),
            pair_no[:, :].rearrange("p (c t) -> p c t", t=NT).unsqueeze(1).to_broadcast([P, SLOTS, NPAIR, NT]), ALU.is_equal))
        w4 = work[:, :].rearrange("p (h k c) -> p h k c", h=HEADS, k=TOPK)
        ev[("picks", m)] = dve.step("picks", [k] + [ev[("cid", m, t)] for t in range(NT)], lambda: V.tensor_tensor(
            w4, w4, cid[:, :, :, :].rearrange("p h c t -> p h (c t)").unsqueeze(2).to_broadcast([P, HEADS, TOPK, NPAIR * NT]),
            ALU.mult))

    def pick_gates(m):
        TH = NT * HEADS
        g4 = gate[:, :, :].rearrange("p t (h k) -> p (t h) k", k=TOPK)
        e = ev[("shift", m)] = pool.step("shift", [ev[("pairs", m, NT - 1)], get(("gate_pe", m - 1))], lambda: G.tensor_tensor(
            g4, top[:, :, 0:TOPK], top[:, :, 0:1].to_broadcast([P, TH, TOPK]), ALU.subtract))
        f = act.step("exp", [e], lambda: S.activation(g4, g4, ACT.Exp))
        g = dve.step("gsum", [f], lambda: V.tensor_reduce(gsum[:, :], g4, AX.X, ALU.add))
        h = dve.step("grecip", [g], lambda: V.reciprocal(gsum[:, :], gsum[:, :]))
        ev[("gate", m)] = pool.step("gate", [h], lambda: G.tensor_tensor(
            g4, g4, gsum[:, :].unsqueeze(2).to_broadcast([P, TH, TOPK]), ALU.mult))

    def turn_picks(m):
        bank = misc()
        pk = work[:, :].rearrange("p (s c t) -> p s c t", s=SLOTS, c=NPAIR)

        def ids_pe():
            for t in range(NT):
                for c in range(NPAIR):
                    last = T.matmul(bank.t[0:SLOTS, t * P:(t + 1) * P], pk[:, :, c, t], ident16[:, :],
                                    start=c == 0, stop=c == NPAIR - 1)
            return last
        a = ev[("picks_pe", m)] = pe.step("picks", [ev[("picks", m)]] + bank.free, ids_pe)
        b = dve.step("eid", [a], lambda: V.tensor_scalar(eid[:, 0, :], bank.t[0:SLOTS, 0:C], 2048.0, None, ALU.add))
        bank.free = [b]

        def fields():
            V.tensor_scalar(eid[:, 1, :], eid[:, 0, :], 6, None, ALU.logical_shift_right)
            V.tensor_scalar(eid[:, 2, :], eid[:, 0, :], 1, None, ALU.bitwise_and)
            return V.tensor_scalar(eid[:, 3, :], eid[:, 0, :], 1, NR - 1, ALU.logical_shift_right, ALU.bitwise_and)
        c = dve.step("fields", [b], fields)
        ev[("qid", m)] = dve.step("qid", [c, get(("ohq", m - 1))], lambda: V.scalar_tensor_tensor(
            qid[:, :], eid[:, 2, :], float(NSQ), eid[:, 1, :], ALU.mult, ALU.add))
        ev[("fields", m)] = c

    def turn_r(m):
        ev[("rid", m)] = dve.step("rid", [ev[("fields", m)], get(("ohr", m - 2, NT - 1))],
                                  lambda: V.tensor_copy(rid[:, m % 2, :], eid[:, 3, :]))

    def turn_gates(m):
        bank = misc()

        def gates_pe():
            for t in range(NT):
                last = T.transpose(bank.t[0:SLOTS, t * P:(t + 1) * P], gate[:, t, :], ident[:, :])
            return last
        a = ev[("gate_pe", m)] = pe.step("gate", [ev[("gate", m)], consts] + bank.free, gates_pe)
        b = act.step("gateT", [a, get(("gsplit", m - 1))], lambda: S.mul(gateT[:, :], bank.t[0:SLOTS, 0:C], GATE_SCALE))
        bank.free = [b]
        c = act.step("ghi", [b, get(("ohr", m - 2, NT - 1))], lambda: S.copy(ghi[:, m % 2, :], gateT[:, :]))
        ev[("gsplit", m)] = dve.step("glo", [c], lambda: V.tensor_tensor(glo[:, m % 2, :], gateT[:, :], ghi[:, m % 2, :], ALU.subtract))

    def onehot_r(m, t):
        tok = slice(t * P, (t + 1) * P)
        free = [get(("gates_pe", m, t - 1) if t else ("gates_pe", m - 1, NT - 1))]

        def hot():
            for r in range(NR):
                last = V.tensor_scalar(ohr_lo[:, r, :], rid[:, m % 2, tok], float(r), None, ALU.is_equal)
            return last
        a = dve.step("ohr", [ev[("rid", m)]] + free, hot)
        b = dve.step("ohr_hi", [a, ev[("gsplit", m)]], lambda: V.tensor_tensor(
            ohr_hi[:, :, :], ohr_lo[:, :, :], ghi[:, m % 2, tok].unsqueeze(1).to_broadcast([SLOTS, NR, P]), ALU.mult))
        ev[("ohr", m, t)] = dve.step("ohr_lo", [b], lambda: V.tensor_tensor(
            ohr_lo[:, :, :], ohr_lo[:, :, :], glo[:, m % 2, tok].unsqueeze(1).to_broadcast([SLOTS, NR, P]), ALU.mult))

    def onehot_q(m):
        def hot():
            for q in range(NQ):
                last = V.tensor_scalar(ohq[:, q, :], qid[:, :], float(q), None, ALU.is_equal)
            return last
        ev[("ohq", m)] = dve.step("ohq", [ev[("qid", m)], get(("gates_pe", m - 1, NT - 1))], hot)

    def gate_matrix(m, t):
        for g in range(P // GROUP):
            bank = sbank[g % 2]

            def mm(g=g, bank=bank):
                for n in range(GROUP):
                    tok = g * GROUP + n
                    dst = bank.t[:, n * NR:(n + 1) * NR]
                    T.matmul(dst, ohq[:, :, t * P + tok], ohr_hi[:, :, tok], start=True, stop=False)
                    last = T.matmul(dst, ohq[:, :, t * P + tok], ohr_lo[:, :, tok], start=False, stop=True)
                return last
            a = pe.step("gates", [ev[("ohq", m)], ev[("ohr", m, t)]] + bank.free, mm)
            tok0 = t * P + g * GROUP
            b = act.step("gates", [a, get(("mix", m - 1))], lambda bank=bank, tok0=tok0: S.mul(
                gates[:, :, tok0:tok0 + GROUP], bank.t[:, :].rearrange("p (n r) -> p r n", r=NR), 1.0 / GATE_SCALE))
            bank.free = [b]
        ev[("gates_pe", m, t)] = a
        ev[("gates", m)] = b

    def split_down(m, p):
        slot = wd_split[p % WD_SLOTS]
        src = wdown[:, :, 2 * p:2 * p + 2, :]
        free = get(("down", m, p - WD_SLOTS)) if p >= WD_SLOTS else get(("down_pe", m - 1))
        a = act.step("wd_hi", [wd_in, free], lambda: S.copy(slot[:, 0, :, :, :], src))
        ev[("wd_split", m, p)] = pool.step("wd_lo", [a], lambda: G.tensor_tensor(
            slot[:, 1, :, :, :], src, slot[:, 0, :, :, :].bitcast(F32), ALU.subtract))

    def experts(m, between):
        mixed, wup_in = {}, {}
        for p in range(NR // 2 + LAG):
            for work_of_next in between.get(p, []):
                work_of_next()
            if p < NR // 2:
                bank, slot = hbank[p % 2], p % 4
                n = m * (NR // 2) + p

                def down(p=p, bank=bank):
                    wd = wd_split[p % WD_SLOTS]
                    for j in range(2):
                        parts = [(wd[:, w_part, k, j, :], x_part[:, m % 3, k, :]) for k in range(KD)
                                 for w_part, x_part in ((0, xT_hi), (0, xT_lo), (1, xT_hi))]
                        for i, (a, c) in enumerate(parts):
                            last = T.matmul(bank.t[:, j * C:(j + 1) * C], a, c, start=i == 0, stop=i == len(parts) - 1)
                    return last
                a = ev[("down", m, p)] = pe.step("down", [ev[("xT_split", m)], ev[("wd_split", m, p)]] + bank.free, down)
                scored = get(("score_pe", m + 2)) if p < 4 else None
                split = get(("xT_split", m + 2)) if p == 3 else None
                b = act.step("gelu", [a, get(("up", n - 4)), scored, split], lambda bank=bank, slot=slot: S.activation(
                    hid[:, slot, :, :], bank.t[:, :].rearrange("p (j c) -> p j c", j=2), ACT.Gelu))
                bank.free = [b]
                mixed[p] = pool.step("mix", [b, ev[("gates", m)]], lambda p=p, slot=slot: G.tensor_tensor(
                    hid[:, slot, :, :], hid[:, slot, :, :], gates[:, 2 * p:2 * p + 2, :], ALU.mult))
                if p + WD_SLOTS < NR // 2:
                    split_down(m, p + WD_SLOTS)
                wup_in[p] = sp.dma(f"wup{slot}", [get(("up", n - 4))], lambda p=p, slot=slot: nc.sync.dma_start(
                    wup[:, slot, :, :], w["wup"][:, 2 * p:2 * p + 2, :]))
            if p >= LAG:
                u = p - LAG

                def up(u=u):
                    for j in range(2):
                        for t in range(NT):
                            last = T.matmul(abank[t].t[:, 0:D], hid[:, u % 4, j, t * P:(t + 1) * P], wup[:, u % 4, j, :],
                                            start=u == 0 and j == 0, stop=u == NR // 2 - 1 and j == 1)
                    return last
                free = abank[0].free if u == 0 else []
                ev[("up", m * (NR // 2) + u)] = pe.step("up", [mixed[u], wup_in[u]] + free, up)
        ev[("mix", m)] = mixed[NR // 2 - 1]
        ev[("down_pe", m)] = a
        ev[("acc", m)] = ev[("up", m * (NR // 2) + NR // 2 - 1)]

    def finish(m):
        moments(1, m, lambda t: abank[t].t[:, 0:D], [ev[("acc", m)]])

    def store(m):
        a = sp.dma("x1t", [get(("res", m - 1)), x1_ready],
                   lambda: nc.sync.dma_start(x1t[:, :, :], x1_view[m]))
        e = normalise(1, m, lambda t: abank[t].t[:, 0:D], y, [get(("out", m - 1))])
        for b in abank:
            b.free = [e]
        r = ev[("res", m)] = pool.step("res", [a, e], lambda: G.tensor_tensor(y[:, :, :], y[:, :, :], x1t[:, :, :], ALU.add))
        ev[("out", m)] = sp.dma("out", [r], lambda: nc.sync.dma_start(out_view[m], y[:, :, :]))

    def has(m):
        return 0 <= m < chunks

    for m in range(-3, chunks + 1):
        one, two, three = has(m + 1), has(m + 2), has(m + 3)
        if one:
            pick_gates(m + 1)
        if has(m):
            gate_matrix(m, 0)
            onehot_r(m, 1)
        if two:
            turn_x(m + 2)
        if one:
            turn_picks(m + 1)
            turn_r(m + 1)
        if has(m - 1):
            finish(m - 1)
            root(1, m - 1)
        if one:
            turn_gates(m + 1)
        if has(m - 1):
            store(m - 1)
        if two:
            scores(m + 2)
            lists_top(m + 2, 0)
            numbers(m + 2, 0)
        if has(m):
            for p in range(WD_SLOTS):
                split_down(m, p)
            gate_matrix(m, 1)
        if three:
            load(m + 3)
        if one:
            onehot_q(m + 1)
            onehot_r(m + 1, 0)
        if two:
            lists_top(m + 2, 1)
            numbers(m + 2, 1)
        between = {6: [(three, lambda: root(0, m + 3))], 4: [(two, lambda: pair_sums(m + 2, 0))], 5: [(two, lambda: pair_numbers(m + 2, 0))],
                   14: [(two, lambda: pair_sums(m + 2, 1)), (two, lambda: pair_numbers(m + 2, 1)),
                        (two, lambda: pairs_top(m + 2, 0)), (two, lambda: pairs_top(m + 2, 1)), 
                        (two, lambda: pick(m + 2)), (three, lambda: norm_in(m + 3))]}
        between = {p: [f for wanted, f in fs if wanted] for p, fs in between.items()}
        if has(m):
            experts(m, between)
        else:
            for fs in between.values():
                for f in fs:
                    f()
    sp.last_wait([ev[("out", chunks - 1)]])
    return pe, act, dve, pool, sp


CA = 512
TA = CA // P
MAGIC = 12582912.0
TWO_PI = (6.28125, 0.0019350051879882812, 3.0199159819567534e-07)
PI = 3.1415925


def attention_phase(nc, ctx, sems, seqs, length, x_dram, x1_dram, w):
    sb = lambda name, shape, dt=F32: ctx.enter_context(nc.sbuf_tensor(name, shape, dt))
    ps = lambda name: Bank(ctx.enter_context(nc.psum_tensor(name, [P, 512], F32)))
    pe, act, dve, pool, sp = (Queue(nc, sems, t) for t in ("pe_a", "act_a", "dve_a", "pool_a", "sp_a"))
    T, V, S, G = nc.tensor, nc.vector, nc.scalar, nc.gpsimd
    chunks = seqs * length // CA

    ident, tri, last_row, ones = (sb(f"a_{n}", [P, P]) for n in ("ident", "tri", "last_row", "ones"))
    wproj = sb("a_wproj", [P, KD, 3 * D])
    wg1 = sb("a_wg1", [P, 2 * KD, D])
    wb1 = sb("a_wb1", [P, KD, P])
    wo = sb("a_wo", [P, KD, D])
    wg2 = sb("a_wg2", [P, KD])
    wb2 = sb("a_wb2", [P, 2])
    cols = sb("a_cols", [P, 7])
    head_b = sb("a_head_b", [P, 3])
    brow = sb("a_brow", [3, 5 * D])
    brest = sb("a_brest", [3, 5 * D])
    bpart = sb("a_bpart", [3, 3, 5 * D], BF16)
    bsum = sb("a_bsum", [3, 5 * D])
    bsplit = sb("a_bsplit", [3, 5 * D], BF16)
    row_mask = sb("a_row_mask", [3, 3])
    ones3 = sb("a_ones3", [3, P], BF16)
    minus_half = sb("a_minus_half", [P, TA])
    half_pi = sb("a_half_pi", [P, 1])
    ph = sb("a_ph", [P, TA * D])
    turns = sb("a_turns", [P, TA * D])
    cs = sb("a_cs", [P, 2, TA, 2, D])
    x = sb("a_x", [P, 4, TA, D])
    xn = sb("a_xn", [P, 4, TA, D])
    xT = sb("a_xT", [P, 4, KD, CA + 1])
    th = sb("a_th", [P, TA, D])
    tha = sb("a_tha", [P, TA, D])
    key = sb("a_key", [P, 2, TA, 2, D])
    keysh = sb("a_keysh", [P, 2, TA, 2, D])
    gh = sb("a_gh", [P, 3, CA])
    z = sb("a_z", [P, TA, 3])
    zmax = sb("a_zmax", [P, TA])
    den = sb("a_den", [P, 2, TA])
    gates = sb("a_gates", [P, 2, TA])
    gcum = sb("a_gcum", [P, 4, TA])
    fac = sb("a_fac", [P, 2, 2, TA])
    u = sb("a_u", [P, 2, 4 * D])
    carry = sb("a_carry", [P, seqs, 4 * D])
    prod = sb("a_prod", [P, 2, 2, 2, D])
    ret = sb("a_ret", [P, 2, 2, D])
    bl = sb("a_bl", [P, 2, TA, D])
    lnT = sb("a_lnT", [P, KD, CA])
    y = sb("a_y", [P, TA, D])
    stat = sb("a_stat", [P, 3, TA, 6])
    mv = sb("a_mv", [P, 3, TA, 2])
    rstd = sb("a_rstd", [P, 3, TA])
    tbank = [ps("a_ps_t0"), ps("a_ps_t1")]
    fbank = [ps("a_ps_f0"), ps("a_ps_f1")]
    pbank = [ps("a_ps_p0"), ps("a_ps_p1")]
    cbank = [ps("a_ps_c0"), ps("a_ps_c1")]
    turn_of = {"t": 0, "f": 0, "p": 0}

    def bank_of(kind):
        turn_of[kind] += 1
        return {"t": tbank, "f": fbank, "p": pbank}[kind][turn_of[kind] % 2]

    ev = {}
    get = ev.get

    loaded = None
    by_k = lambda a: a.rearrange("(k p) n -> p k n", p=P)
    for dst, src in ((ident[:, :], w["ident"]), (tri[:, :], w["tri"]), (last_row[:, :], w["last_row"]), (ones[:, :], w["ones"]),
                     (wproj[:, :, 0:D], by_k(w["wpv"])), (wproj[:, :, D:2 * D], by_k(w["wkv"])),
                     (wproj[:, :, 2 * D:3 * D], by_k(w["wk"])), (wg1[:, :, :], by_k(w["wg1"])), (wb1[:, :, :], by_k(w["wb1"])),
                     (wo[:, :, :], by_k(w["wo"])), (wg2[:, :], w["wg2"]), (wb2[:, :], w["wb2"]), (cols[:, :], w["cols"]),
                     (head_b[:, :], w["head_b"]), (brow[:, :], w["brow"]), (row_mask[:, :], w["row_mask"])):
        loaded = sp.dma("weights", [], lambda dst=dst, src=src: nc.sync.dma_start(dst, src))

    def set_constants():
        G.memset(minus_half[:, :], -0.5)
        G.memset(half_pi[:, :], PI / 2)
        G.memset(ones3[:, :], 1.0)
        for b in range(seqs):
            G.memset(keysh[0:1, b, 0, :, :], 0.0)
        return G.memset(carry[:, :, :], 0.0)
    constants = pool.step("constants", [], set_constants)

    s = dve.step("bias0", [loaded], lambda: V.tensor_copy(bpart[:, 0, :], brow[:, :]))
    s = dve.step("bias1", [s], lambda: V.tensor_tensor(brest[:, :], brow[:, :], bpart[:, 0, :], ALU.subtract))
    s = dve.step("bias2", [s], lambda: V.tensor_copy(bpart[:, 1, :], brest[:, :]))
    s = dve.step("bias3", [s], lambda: V.tensor_tensor(brest[:, :], brest[:, :], bpart[:, 1, :], ALU.subtract))
    s = dve.step("bias4", [s], lambda: V.tensor_copy(bpart[:, 2, :], brest[:, :]))
    s = dve.step("bias5", [s], lambda: V.tensor_scalar(bsum[:, :], bpart[:, 0, :], row_mask[:, 0:1], None, ALU.mult))
    s = dve.step("bias6", [s], lambda: V.scalar_tensor_tensor(bsum[:, :], bpart[:, 1, :], row_mask[:, 1:2], bsum[:, :],
                                                              ALU.mult, ALU.add))
    bias = dve.step("bias7", [s], lambda: V.scalar_tensor_tensor(bsplit[:, :], bpart[:, 2, :], row_mask[:, 2:3], bsum[:, :],
                                                                 ALU.mult, ALU.add))

    def where(n):
        j, b = divmod(n, seqs)
        rows = slice(b * length + j * CA, b * length + (j + 1) * CA)
        return j, b, rows

    def rows_of(dram, rows):
        return dram[rows, :].rearrange("(t p) d -> p t d", p=P)

    def moments(which, n, src, ready):
        def stats():
            for t in range(TA):
                last = V.bn_stats(stat[:, which, t, :], src(t))
            return last
        a = dve.step(f"stats{which}", ready + [get((f"aggr{which}", n - 1))], stats)

        def aggr():
            for t in range(TA):
                last = V.bn_aggr(mv[:, which, t, :], stat[:, which, t, :])
            return last
        b = ev[(f"aggr{which}", n)] = dve.step(f"aggr{which}", [a, get((f"norm{which}", n - 1))], aggr)
        c = pool.step(f"eps{which}", [b, get((f"norm{which}", n - 1))],
                      lambda: G.tensor_scalar(rstd[:, which, :], mv[:, which, :, 1], EPS, None, ALU.add))
        ev[(f"rstd{which}", n)] = pool.step(f"rstd{which}", [c, constants],
                      lambda: G.tensor_tensor(rstd[:, which, :], rstd[:, which, :], minus_half[:, :], ALU.pow))

    def normalise(which, n, src, dst, dst_free):
        def norm():
            for t in range(TA):
                last = V.tensor_scalar(dst(t), src(t), mv[:, which, t, 0:1], rstd[:, which, t:t + 1], ALU.subtract, ALU.mult)
            return last
        e = ev[(f"norm{which}", n)] = dve.step(f"norm{which}", [ev[(f"rstd{which}", n)]] + dst_free, norm)
        return e

    def load(n):
        j, b, rows = where(n)
        ev[("x", n)] = sp.dma(f"x{n % 4}", [get(("x1", n - 4))],
                                  lambda: nc.sync.dma_start(x[:, n % 4, :, :], rows_of(x_dram, rows)))

    def moments_in(n):
        moments(0, n, lambda t: x[:, n % 4, t, :], [ev[("x", n)]])

    def norm_in(n):
        normalise(0, n, lambda t: x[:, n % 4, t, :], lambda t: xn[:, n % 4, t, :], [get(("y", n - 4))])

    def load_phases(n):
        j = n // seqs
        if n % seqs == 0:
            ev[("ph", j)] = sp.dma("ph", [get(("cs", j - 1))], lambda: nc.sync.dma_start(
                ph[:, :].rearrange("p (t d) -> p t d", t=TA), rows_of(w["phases"], slice(j * CA, (j + 1) * CA))))

    def reduce_phases(n):
        j = n // seqs
        if n % seqs:
            return
        b = dve.step("turns", [ev[("ph", j)], get(("cs", j - 1))], lambda: V.tensor_scalar(
            turns[:, :], ph[:, :], 0.15915494309189535, MAGIC, ALU.mult, ALU.add))
        b = dve.step("turns", [b], lambda: V.tensor_scalar(turns[:, :], turns[:, :], MAGIC, None, ALU.subtract))
        for part in TWO_PI:
            b = dve.step("reduce", [b], lambda part=part: V.scalar_tensor_tensor(
                ph[:, :], turns[:, :], -part, ph[:, :], ALU.mult, ALU.add))
        ev[("reduced", j)] = dve.step("clamp", [b], lambda: V.tensor_scalar(ph[:, :], ph[:, :], -PI, PI, ALU.max, ALU.min))

    def waves(n):
        j, slot = n // seqs, n // seqs % 2
        if n % seqs:
            return
        c = act.step("ph_abs", [ev[("reduced", j)]], lambda: S.activation(turns[:, :], ph[:, :], ACT.Abs))
        four = lambda a: a.rearrange("p (t d) -> p t d", t=TA)

        def both():
            S.activation(cs[:, slot, :, 1, :], four(ph[:, :]), ACT.Sin)
            return S.activation(cs[:, slot, :, 0, :], four(turns[:, :]), ACT.Sin, bias=half_pi[:, :], scale=-1.0)
        ev[("cs", j)] = act.step("cs", [c, constants, get(("prod", (j - 2) * seqs + seqs - 1, TA - 1))], both)

    def turn_x(n):
        j, b, _ = where(n)
        slot = n % 4
        done = []
        for k in range(KD):
            bank = bank_of("t")

            def tr(k=k, bank=bank):
                for t in range(TA):
                    last = T.transpose(bank.t[:, t * P:(t + 1) * P], xn[:, slot, t, k * P:(k + 1) * P], ident[:, :])
                return last
            a = pe.step("xT", [ev[("norm0", n)], loaded] + bank.free, tr)
            c = act.step("xT", [a, get(("pv_pe", n - 4))], lambda k=k, bank=bank: S.copy(xT[:, slot, k, 1:CA + 1], bank.t[:, :]))
            bank.free = [c]
        if j:
            d = act.step("x_before", [c, ev[("xT", n - seqs)]],
                         lambda: S.copy(xT[:, slot, :, 0:1], xT[:, (n - seqs) % 4, :, CA:CA + 1]))
        else:
            d = pool.step("x_before", [], lambda: G.memset(xT[:, slot, :, 0:1], 0.0))
        ev[("xT", n)] = c
        ev[("x_before", n)] = d

    def keys(n):
        j, b, _ = where(n)
        slot = n % 2
        for half in range(2):
            bank = bank_of("f")

            def proj(half=half, bank=bank):
                T.matmul(bank.t[:, 0:D], ones3[:, :], bsplit[:, 2 * D:3 * D], start=True, stop=False, skip_group_check=True)
                T.matmul(bank.t[:, D:2 * D], ones3[:, :], bsplit[:, 2 * D:3 * D], start=False, stop=False, skip_group_check=True)
                for i in range(2):
                    t = 2 * half + i
                    for k in range(KD):
                        last = T.matmul(bank.t[:, i * D:(i + 1) * D], xT[:, n % 4, k, 1 + t * P:1 + (t + 1) * P],
                                        wproj[:, k, 2 * D:3 * D], start=False, stop=i == 1 and k == KD - 1, skip_group_check=True)
                return last
            a = pe.step("keys", [ev[("xT", n)], bias, constants] + bank.free, proj)
            c = act.step("tanh", [a, get(("key", n - 1))], lambda half=half, bank=bank: S.activation(
                th[:, 2 * half:2 * half + 2, :], bank.t[:, :].rearrange("p (t d) -> p t d", t=2), ACT.Tanh))
            bank.free = [c]
        ev[("tanh", n)] = c

    def key_waves(n):
        j, b, _ = where(n)
        slot = n % 2
        d = act.step("th_abs", [ev[("tanh", n)]], lambda: S.activation(tha[:, :, :], th[:, :, :], ACT.Abs))

        def both():
            S.activation(key[:, slot, :, 1, :], th[:, :, :], ACT.Sin, scale=PI)
            return S.activation(key[:, slot, :, 0, :], tha[:, :, :], ACT.Sin, bias=half_pi[:, :], scale=-PI)
        e = ev[("key", n)] = act.step("key", [d, constants, get(("prod", n - 2, TA - 1)), get(("keysh_in", n - 2)), get(("key_end", n - 2))], both)
        free = get(("u", n - 2, TA - 1))
        moves = [(keysh[1:113, slot, :, :, :], key[0:112, slot, :, :, :]),
                 (keysh[113:128, slot, :, :, :], key[112:127, slot, :, :, :]),
                 (keysh[0:1, slot, 1:TA, :, :], key[127:128, slot, 0:TA - 1, :, :])]
        for dst, src in moves:
            f = sp.dma(f"keysh{slot}", [e, free], lambda dst=dst, src=src: nc.sync.dma_start(dst, src))
        if j:
            f = sp.dma(f"keysh{slot}", [free, ev[("key_end", n - seqs)]],
                       lambda: nc.sync.dma_start(keysh[0:1, slot, 0, :, :], key_end[0:1, b, :, :]))
        ev[("key_end", n)] = sp.dma(f"key_end{b}", [e, f],
                                        lambda: nc.sync.dma_start(key_end[0:1, b, :, :], key[127:128, slot, TA - 1, :, :]))
        ev[("keysh_in", n)] = f

    key_end = sb("a_key_end", [1, seqs, 2, D])

    def gating(n):
        j, b, _ = where(n)
        slot = n % 4
        for m in range(3):
            bank = bank_of("f")

            def hidden(m=m, bank=bank):
                if m < 2:
                    parts = [(wg1[:, k, m * P:(m + 1) * P], xT[:, slot, k, 1:CA + 1]) for k in range(KD)] + \
                            [(wg1[:, KD + k, m * P:(m + 1) * P], xT[:, slot, k, 0:CA]) for k in range(KD)]
                else:
                    parts = [(wb1[:, k, :], xT[:, slot, k, 1:CA + 1]) for k in range(KD)]
                for i, (a, c) in enumerate(parts):
                    last = T.matmul(bank.t[:, :], a, c, start=i == 0, stop=i == len(parts) - 1)
                return last
            a = pe.step("hidden", [ev[("xT", n)], ev[("x_before", n)], loaded] + bank.free, hidden)
            c = act.step("hidden", [a, get(("logits", n - 1))], lambda m=m, bank=bank: S.activation(
                gh[:, m, :], bank.t[:, :], ACT.Gelu, bias=cols[:, m:m + 1]))
            bank.free = [c]
        ev[("hidden", n)] = c

    def gate_values(n):
        bank = bank_of("f")

        def logits():
            for t in range(TA):
                tok = slice(t * P, (t + 1) * P)
                for m in range(2):
                    T.matmul(bank.t[:, 3 * t:3 * t + 1], gh[:, m, tok], wg2[:, m:m + 1], start=m == 0, stop=m == 1)
                last = T.matmul(bank.t[:, 3 * t + 1:3 * t + 3], gh[:, 2, tok], wb2[:, :], start=True, stop=True)
            return last
        a = ev[("logits", n)] = pe.step("logits", [ev[("hidden", n)]] + bank.free, logits)
        s = dve.step("z", [a, get(("fac", n - 1))], lambda: V.tensor_tensor(
            z[:, :, :], bank.t[:, 0:3 * TA].rearrange("p (t c) -> p t c", c=3),
            head_b[:, :].unsqueeze(1).to_broadcast([P, TA, 3]), ALU.add))
        bank.free = [s]
        s = dve.step("zmax", [s], lambda: V.tensor_tensor(zmax[:, :], z[:, :, 1], z[:, :, 2], ALU.max))

        def shift():
            V.tensor_scalar(z[:, :, 0], z[:, :, 0], -1.0, None, ALU.mult)
            return V.tensor_tensor(z[:, :, 1:3], z[:, :, 1:3], zmax[:, :].unsqueeze(2).to_broadcast([P, TA, 2]), ALU.subtract)
        s = dve.step("zshift", [s], shift)
        s = act.step("exp", [s], lambda: S.activation(z[:, :, :], z[:, :, :], ACT.Exp))

        def sums():
            V.tensor_scalar(den[:, 0, :], z[:, :, 0], 1.0, None, ALU.add)
            return V.tensor_tensor(den[:, 1, :], z[:, :, 1], z[:, :, 2], ALU.add)
        s = dve.step("den", [s], sums)
        s = dve.step("recip", [s], lambda: V.reciprocal(den[:, :, :], den[:, :, :]))

        s = dve.step("gate", [s, get(("u", n - 2, TA - 1)), get(("gcum_pe", n - 2))],
                     lambda: V.tensor_copy(gates[:, n % 2, :], den[:, 0, :]))
        ev[("gate", n)] = s

    def gate_sums(n):
        j, b, _ = where(n)
        gate = ev[("gate", n)]
        bank = bank_of("f")

        def gsum():
            g = gates[:, n % 2, :]
            last = T.matmul(bank.t[:, 0:TA], tri[:, :], g, start=True, stop=False)
            for t in range(TA - 1):
                last = T.matmul(bank.t[:, t + 1:TA], ones[:, :], g[:, t:t + 1].to_broadcast([P, TA - 1 - t]), start=False,
                                stop=not j and t == TA - 2)
            if j:
                last = T.matmul(bank.t[:, 0:TA], last_row[:, :], gcum[:, (n - seqs) % 4, TA - 1:TA].to_broadcast([P, TA]),
                                start=False, stop=True)
            return last
        a = ev[("gcum_pe", n)] = pe.step("gcum", [gate, get(("gcum", n - seqs)) if j else None] + bank.free, gsum)
        s = ev[("gcum", n)] = dve.step("gcum", [a, get(("gcum_pe", n - 2))], lambda: V.tensor_copy(
            gcum[:, n % 4, :], bank.t[:, 0:TA]))
        bank.free = [s]
        s = dve.step("gmax", [s], lambda: V.tensor_scalar(zmax[:, :], gcum[:, n % 4, :], 1.0, None, ALU.max))
        ev[("groot", n)] = pool.step("groot", [s, constants], lambda: G.tensor_tensor(zmax[:, :], zmax[:, :], minus_half[:, :], ALU.pow))

    def gate_factors(n):
        s1 = dve.step("zscale", [ev[("groot", n)]], lambda: V.scalar_tensor_tensor(
            z[:, :, 1:3], z[:, :, 1:3], 1.0 / 16, den[:, 1, :].unsqueeze(2).to_broadcast([P, TA, 2]), ALU.mult, ALU.mult))

        def factors():
            V.tensor_copy(fac[:, n % 2, 0, :], z[:, :, 1])
            return V.tensor_tensor(fac[:, n % 2, 1, :], z[:, :, 2], zmax[:, :], ALU.mult)
        ev[("fac", n)] = dve.step("fac", [s1, get(("blend", n - 2, TA - 1))], factors)

    def values(n, t):
        j, b, _ = where(n)
        bank = bank_of("p")

        def proj():
            T.matmul(bank.t[:, :], ones3[:, :], bsplit[:, 0:2 * D], start=True, stop=False)
            for k in range(KD):
                last = T.matmul(bank.t[:, :], xT[:, n % 4, k, 1 + t * P:1 + (t + 1) * P], wproj[:, k, 0:2 * D],
                                start=False, stop=k == KD - 1)
            return last
        a = ev[("pv_pe", n)] = pe.step("values", [ev[("xT", n)], bias, constants] + bank.free, proj)
        i = (n * TA + t) % 2
        twice = lambda v: v.unsqueeze(1).to_broadcast([P, 2, D])

        def terms():
            V.tensor_tensor(u[:, i, 0:2 * D].rearrange("p (s d) -> p s d", s=2), cs[:, j % 2, t, :, :],
                            twice(bank.t[:, 0:D]), ALU.mult)
            return V.scalar_tensor_tensor(u[:, i, 2 * D:4 * D].rearrange("p (s d) -> p s d", s=2), twice(bank.t[:, D:2 * D]),
                                          gates[:, n % 2, t:t + 1], keysh[:, n % 2, t, :, :], ALU.mult, ALU.mult)
        c = ev[("u", n, t)] = dve.step("u", [a, ev[("cs", j)], ev[("gate", n)], ev[("keysh_in", n)],
                                             get(("sum_pe", n * TA + t - 2))], terms)
        bank.free = [c]

    def sums(n, t):
        j, b, _ = where(n)
        i = (n * TA + t) % 2
        first = j == 0 and t == 0

        def cum():
            for h in range(2):
                last = T.matmul(cbank[h].t[:, :], tri[:, :], u[:, i, h * 512:(h + 1) * 512], start=True, stop=first)
            if not first:
                for h in range(2):
                    last = T.matmul(cbank[h].t[:, :], last_row[:, :], carry[:, b, h * 512:(h + 1) * 512], start=False, stop=True)
            return last
        a = ev[("sum_pe", n * TA + t)] = pe.step("sums", [ev[("u", n, t)], loaded, ev.get(("carry", b)), constants] + cbank[0].free, cum)

        def keep():
            for h in range(2):
                last = S.copy(carry[96:128, b, h * 512:(h + 1) * 512], cbank[h].t[96:128, :])
            return last
        c = ev[("carry", b)] = act.step("carry", [a], keep)

        def back():
            V.tensor_tensor(prod[:, i, 0, :, :], cbank[0].t[:, :].rearrange("p (s d) -> p s d", s=2), cs[:, j % 2, t, :, :], ALU.mult)
            return V.tensor_tensor(prod[:, i, 1, :, :], cbank[1].t[:, :].rearrange("p (s d) -> p s d", s=2),
                                   key[:, n % 2, t, :, :], ALU.mult)
        d = ev[("prod", n, t)] = dve.step("prod", [c, get(("ret", n * TA + t - 2))], back)
        for bank in cbank:
            bank.free = [d]
        e = ev[("ret", n * TA + t)] = pool.step("ret", [d, get(("blend", n * TA + t - 2))], lambda: G.tensor_tensor(
            ret[:, i, :, :], prod[:, i, :, 0, :], prod[:, i, :, 1, :], ALU.add))
        f = pool.step("ret_pos", [e, ev[("fac", n)]], lambda: G.tensor_scalar(
            ret[:, i, 0, :], ret[:, i, 0, :], fac[:, n % 2, 0, t:t + 1], None, ALU.mult))
        ev[("ret_pos", n, t)] = f

    def blend(n, t):
        i = (n * TA + t) % 2
        g = dve.step("blend", [ev[("ret_pos", n, t)], get(("norm1", n - 2))], lambda: V.scalar_tensor_tensor(
            bl[:, n % 2, t, :], ret[:, i, 1, :], fac[:, n % 2, 1, t:t + 1], ret[:, i, 0, :], ALU.mult, ALU.add))
        ev[("blend", n, t)] = ev[("blend", n * TA + t)] = g

    def blend_moments(n):
        moments(1, n, lambda t: bl[:, n % 2, t, :], [ev[("blend", n, TA - 1)]])

    def blend_norm(n):
        normalise(1, n, lambda t: bl[:, n % 2, t, :], lambda t: bl[:, n % 2, t, :], [])

    def turn_blend(n):
        for k in range(KD):
            bank = bank_of("t")

            def tr(k=k, bank=bank):
                for t in range(TA):
                    last = T.transpose(bank.t[:, t * P:(t + 1) * P], bl[:, n % 2, t, k * P:(k + 1) * P], ident[:, :])
                return last
            a = ev[("lnT_pe", n)] = pe.step("lnT", [ev[("norm1", n)]] + bank.free, tr)
            c = act.step("lnT", [a, get(("wo_pe", n - 1)), loaded], lambda k=k, bank=bank: S.activation(
                lnT[:, k, :], bank.t[:, :], ACT.Identity, bias=cols[:, 5 + k:6 + k], scale=cols[:, 3 + k:4 + k]))
            bank.free = [c]
        ev[("lnT", n)] = c

    def project_out(n):
        c = ev[("lnT", n)]
        for half in range(2):
            bank = bank_of("t")

            def proj(half=half, bank=bank):
                T.matmul(bank.t[:, :], ones3[:, :], bsplit[:, 3 * D:5 * D], start=True, stop=False, skip_group_check=True)
                for i in range(2):
                    t = 2 * half + i
                    for k in range(KD):
                        last = T.matmul(bank.t[:, i * D:(i + 1) * D], lnT[:, k, t * P:(t + 1) * P], wo[:, k, :],
                                        start=False, stop=i == 1 and k == KD - 1, skip_group_check=True)
                return last
            a = pe.step("wo", [c, bias] + bank.free, proj)
            d = dve.step("y", [a, get(("x1_out", n - 1))], lambda half=half, bank=bank: V.tensor_tensor(
                y[:, 2 * half:2 * half + 2, :], bank.t[:, :].rearrange("p (t d) -> p t d", t=2),
                xn[:, n % 4, 2 * half:2 * half + 2, :], ALU.add))
            bank.free = [d]
        ev[("wo_pe", n)] = a
        ev[("y", n)] = d
        moments(2, n, lambda t: y[:, t, :], [d])

    def residual(n):
        j, b, rows = where(n)
        e = normalise(2, n, lambda t: y[:, t, :], lambda t: y[:, t, :], [])
        f = ev[("x1", n)] = pool.step("x1", [e, ev[("x", n)]], lambda: G.tensor_tensor(
            y[:, :, :], y[:, :, :], x[:, n % 4, :, :], ALU.add))
        ev[("x1_out", n)] = sp.dma("x1", [f], lambda: nc.sync.dma_start(rows_of(x1_dram, rows), y[:, :, :]))

    def has(n):
        return 0 <= n < chunks

    for n in range(-2, chunks + 1):
        stages = [(n, values, 0), (n + 2, load), (n + 2, load_phases), (n + 1, turn_x), (n, values, 1), (n, gate_factors), (n - 1, blend, TA - 1),
                  (n - 1, blend_moments), (n, sums, 0),
                  (n + 2, moments_in), (n, values, 2), (n - 1, blend_norm), (n, blend, 0), (n + 1, keys), (n, sums, 1), (n + 2, norm_in),
                  (n + 1, key_waves), (n + 2, reduce_phases),
                  (n, blend, 1),
                  (n - 1, turn_blend), (n + 1, gating), (n, values, 3), (n, sums, 2), (n - 1, project_out),
                  (n, blend, 2), (n + 1, gate_values), (n - 1, residual), (n, sums, 3), (n + 1, waves),
                  (n + 1, gate_sums)]
        for chunk, stage, *tile in stages:
            if 0 <= chunk < chunks:
                stage(chunk, *tile)
    sp.last_wait([ev[("x1_out", chunks - 1)]])
    return (pe, act, dve, pool, sp), ev[("x1_out", chunks - 1)]


def build(nc, x, phases, wpv, wkv, wk, wg1, wg2, wb1, wb2, wo, cols, head_b, brow, row_mask, ident, tri, last_row, ones,
          ident16, wq, bq, keys, wdown, wup, pair_no, out, seqs, length):
    x1 = nc.dram_tensor("x1_between", [seqs * length, D], F32, kind="Internal").ap()
    with ExitStack() as sems:
        with ExitStack() as memory:
            queues, x1_written = attention_phase(
                nc, memory, sems, seqs, length, x, x1,
                dict(phases=phases, wpv=wpv, wkv=wkv, wk=wk, wg1=wg1, wg2=wg2, wb1=wb1, wb2=wb2, wo=wo, cols=cols, head_b=head_b,
                     brow=brow, row_mask=row_mask, ident=ident, tri=tri, last_row=last_row, ones=ones))
            in_blocks(nc, *queues)
        with ExitStack() as memory:
            queues = experts_phase(
                nc, memory, sems, seqs * length // C, x1, out,
                dict(ident=ident, ident16=ident16, pair_no=pair_no, keys=keys, bq=bq, wq=wq, wdown=wdown, wup=wup), x1_written)
            in_blocks(nc, *queues)


def kernel(**inputs):
    import numpy as np
    import concourse.bacc as bacc
    from concourse.bass_utils import run_bass_kernel_spmd

    a = {k.removeprefix("L0_"): np.asarray(v) for k, v in inputs.items()}
    x = a["attn_x"]
    seqs, length, width = x.shape
    by_feature = lambda v: v.reshape(-1, P).T
    in_rows = lambda v, n: np.tile(v, (n, 1))

    def experts_by_qr(table):
        return table[:NSQ * NSQ].reshape(NSQ, NR, 2, width)

    k1, k2 = a["ffn_K1"], a["ffn_K2"]
    half = k1.shape[1]
    keys = np.zeros((P, 4 * NSQ), k1.dtype)
    for i, k in enumerate((k1, k2, k1, k2)):
        keys[i * half:(i + 1) * half, i * NSQ:(i + 1) * NSQ] = k.T
    last_row = np.zeros((P, P), x.dtype)
    last_row[-1] = 1
    arrays = dict(
        x=x.reshape(-1, width), phases=a["attn_pos_phases"][:length],
        wpv=a["attn_Wpv"], wkv=a["attn_Wkv"], wk=a["attn_Wk"], wg1=a["attn_Wg1"], wg2=by_feature(a["attn_Wg2"]),
        wb1=a["attn_Wb1"], wb2=a["attn_Wb2"], wo=a["attn_Wo"],
        cols=np.concatenate([by_feature(a[n]) for n in ("attn_bg1", "attn_bb1", "attn_ln_g", "attn_ln_b")], 1),
        head_b=in_rows(np.concatenate([a["attn_bg2"], a["attn_bb2"]]), P),
        brow=in_rows(np.concatenate([a[n] for n in ("attn_bpv", "attn_bkv", "attn_bk", "attn_bo", "attn_bo")]), 3),
        row_mask=np.eye(3, dtype=x.dtype), ident=np.eye(P, dtype=x.dtype), tri=np.triu(np.ones((P, P), x.dtype)),
        last_row=last_row, ones=np.ones((P, P), x.dtype), ident16=np.eye(P, dtype=np.float16),
        wq=a["ffn_Wq"], bq=by_feature(a["ffn_bq"]), keys=keys,
        wdown=experts_by_qr(a["ffn_W_down"]).transpose(3, 1, 2, 0).reshape(width, NR, NQ),
        wup=experts_by_qr(a["ffn_W_up"]).transpose(2, 0, 1, 3).reshape(NQ, NR, width),
        pair_no=in_rows(np.repeat(np.arange(NPAIR), NT).astype(np.float16), P),
    )
    arrays = {k: np.ascontiguousarray(v) for k, v in arrays.items()}
    nc = bacc.Bacc("TRN2", target_bir_lowering=False, num_devices=1,
                   dynamic_dma_scratch_size=1024)
    args = {k: nc.dram_tensor(f"in_{k}", v.shape, mybir.dt.from_np(v.dtype), kind="ExternalInput").ap()
            for k, v in arrays.items()}
    out = nc.dram_tensor("out", [seqs * length, width], F32, kind="ExternalOutput").ap()
    build(nc, out=out, seqs=seqs, length=length, **args)
    got = run_bass_kernel_spmd(nc, [{f"in_{k}": v for k, v in arrays.items()}], core_ids=[0])
    return got.results[0]["out"].reshape(x.shape)
```

```python
from contextlib import ExitStack

from concourse import mybir
from concourse.alu_op_type import AluOpType as ALU

F32, F32R, F16, BF16, U16 = mybir.dt.float32, mybir.dt.float32r, mybir.dt.float16, mybir.dt.bfloat16, mybir.dt.uint16
ACT = mybir.ActivationFunctionType
AX = mybir.AxisListType


class Queue:

    def __init__(self, nc, ctx, tag):
        self.nc, self.ctx, self.tag = nc, ctx, tag
        self.items, self.sems, self.counts = [], {}, {}

    def _step(self, name, waits, make, by):
        if name not in self.sems:
            self.sems[name] = self.ctx.enter_context(self.nc.semaphore(f"{self.tag}_{name}"))
            self.counts[name] = 0
        self.counts[name] += by
        self.items.append(([w for w in waits if w is not None], make, self.sems[name], by))
        return self.sems[name], self.counts[name]

    def step(self, name, waits, make):
        return self._step(name, waits, make, 1)

    def dma(self, name, waits, make):
        return self._step(name, waits, make, 16)

    def last_wait(self, waits):
        self.items.append((waits, None, None, 0))

    def run(self, eng):
        passed = {}
        for waits, make, sem, by in self.items:
            for other, value in waits:
                if passed.get(id(other), 0) < value:
                    eng.wait_ge(other, value)
                    passed[id(other)] = value
            if make is not None:
                make().then_inc(sem, by)
        self.items = []


class Bank:

    def __init__(self, tensor):
        self.t, self.free = tensor, []


def in_blocks(nc, pe, act, dve, pool, sp):
    with nc.Block() as block:
        block.tensor(pe.run)
        block.scalar(act.run)
        block.vector(dve.run)
        block.gpsimd(pool.run)
        block.sync(sp.run)


P = 128
D = 256
KD = D // P
HEADS = 8
NSQ = 64
TOPK = 10
LISTS = 2 * HEADS
SLOTS = HEADS * TOPK
NQ, NR = P, NSQ * NSQ // P
C = 256
NT = C // P
GROUP = 512 // NR
EPS = 1e-5
GATE_SCALE = 1024.0
GONE = -3.0e38
PAIRS = [(0, 1, 10, 0), (1, 1, 5, 10), (2, 1, 3, 15), (3, 2, 2, 18), (5, 5, 1, 22)]
NPAIR = 27
LAG = 3
WD_SLOTS = 3
NQ_ACT, NQ_ACT_PARTS = 20, 5


def experts_phase(nc, ctx, sems, chunks, x1_dram, out_dram, w, x1_ready=None):
    sb = lambda name, shape, dt: ctx.enter_context(nc.sbuf_tensor(name, shape, dt))
    ps = lambda name: Bank(ctx.enter_context(nc.psum_tensor(name, [P, 512], F32)))
    pe, act, dve, pool, sp = (Queue(nc, sems, t) for t in ("pe_b", "act_b", "dve_b", "pool_b", "sp_b"))
    T, V, S, G = nc.tensor, nc.vector, nc.scalar, nc.gpsimd

    ident = sb("b_ident", [P, P], F32)
    ident16 = sb("b_ident16", [P, P], F16)
    pair_no = sb("b_pair_no", [P, NPAIR * NT], F16)
    r_no = sb("b_r_no", [P, NR * 2], F16)
    minus_q = sb("b_minus_q", [P, NQ_ACT], F32)
    minus_half = sb("b_minus_half", [P, NT], F32)
    unscale = sb("b_unscale", [P, 1], F32)
    unused = sb("b_unused", [P, 1], F32)
    wq = sb("b_wq", [P, KD, HEADS * 64], F32)
    bq = sb("b_bq", [P, 4], F32)
    keys = sb("b_keys", [P, 256], F32)
    wdown = sb("b_wdown", [P, KD, NR, NQ], F32)
    wup = sb("b_wup", [P, 4, 2, D], F32)
    x1 = sb("b_x1", [P, NT, D], F32)
    x1t = sb("b_x1t", [P, NT, D], F32)
    xn = sb("b_xn", [P, NT, D], F32)
    xT_hi = sb("b_xT_hi", [P, 3, KD, C], F32R)
    xT_lo = sb("b_xT_lo", [P, 3, KD, C], F32R)
    wd_split = [sb(f"b_wd_split{i}", [P, 2, KD, 2, NQ], F32R) for i in range(WD_SLOTS)]
    work = sb("b_work", [P, SLOTS * NPAIR * NT], F16)
    score = work[:, 0:NT * LISTS * NSQ * 2].bitcast(F32).rearrange("p (t l n) -> p t l n", t=NT, l=LISTS)
    val = sb("b_val", [P, NT, LISTS, 16], F32)
    idx = sb("b_idx", [P, NT, LISTS, 16], U16)
    id1 = sb("b_id1", [P, NT, HEADS, TOPK], F16)
    id2 = sb("b_id2", [P, NT, HEADS, TOPK], F16)
    cand = sb("b_cand", [P, NT, HEADS, NPAIR], F32)
    cid = sb("b_cid", [P, HEADS, NPAIR, NT], F16)
    top = sb("b_top", [P, NT * HEADS, 16], F32)
    pos = sb("b_pos", [P, NT * HEADS, 16], U16)
    posf = sb("b_posf", [P, SLOTS, NT], F16)
    picked = sb("b_picked", [P, NT, SLOTS], F16)
    gate = sb("b_gate", [P, NT, SLOTS], F32)
    gsum = sb("b_gsum", [P, NT * HEADS], F32)
    ghi = sb("b_ghi", [SLOTS, 2, C], F16)
    glo = sb("b_glo", [SLOTS, 2, C], F16)
    gateT = sb("b_gateT", [SLOTS, C], F32)
    eid = sb("b_eid", [SLOTS, 4, C], U16)
    qid = sb("b_qid", [SLOTS, C], F16)
    rid = sb("b_rid", [SLOTS, 2, C], F16)
    ohq = sb("b_ohq", [SLOTS, NQ, C], F16)
    ohr = sb("b_ohr", [SLOTS, 2, NR, P], F16)
    gates = sb("b_gates", [P, NR, C], F32)
    hid = sb("b_hid", [P, 4, 2, C], F32)
    qT = hid[:, 0:2, :, :].rearrange("p a b c -> p (a b) c")
    xT = hid[:, 3, :, :]
    stat = sb("b_stat", [P, 2, NT, 6], F32)
    mv = sb("b_mv", [P, 2, NT, 2], F32)
    rstd = sb("b_rstd", [P, 2, NT], F32)
    y = sb("b_y", [P, NT, D], F32)
    sbank = [ps("b_ps_s0"), ps("b_ps_s1"), ps("b_ps_s2")]
    hbank = [ps("b_ps_h0"), ps("b_ps_h1")]
    abank = ps("b_ps_a")
    mbank = [ps("b_ps_m0"), ps("b_ps_m1")]
    misc_turn = [0]

    def misc():
        misc_turn[0] += 1
        return mbank[misc_turn[0] % 2]

    ev = {}
    get = ev.get

    loads = {}
    for name, dst, src in (("ident", ident, w["ident"]), ("ident16", ident16, w["ident16"]),
                           ("pair_no", pair_no, w["pair_no"]), ("r_no", r_no, w["r_no"]),
                           ("minus_q", minus_q, w["minus_q"]), ("keys", keys, w["keys"]), ("bq", bq, w["bq"])):
        loads[name] = sp.dma("consts", [], lambda d=dst, s=src: nc.sync.dma_start(d[:, :], s))
    consts = loads["bq"]
    wq_in = sp.dma("wq", [], lambda: nc.sync.dma_start(wq[:, :, :], w["wq"].rearrange("(k p) n -> p k n", p=P)))

    def set_constants():
        G.memset(unscale[:, :], 1.0 / GATE_SCALE)
        return G.memset(minus_half[:, :], -0.5)
    half_set = pool.step("half", [], set_constants)

    x1_view = x1_dram.rearrange("(m t p) d -> m p t d", t=NT, p=P)
    out_view = out_dram.rearrange("(m t p) d -> m p t d", t=NT, p=P)

    def moments(which, m, src_of, src_ready):
        def stats():
            for t in range(NT):
                last = V.bn_stats(stat[:, which, t, :], src_of(t))
            return last
        a = dve.step(f"stats{which}", src_ready + [get((f"aggr{which}", m - 1))], stats)

        def aggr():
            for t in range(NT):
                last = V.bn_aggr(mv[:, which, t, :], stat[:, which, t, :])
            return last
        b = ev[(f"aggr{which}", m)] = dve.step(f"aggr{which}", [a, get((f"norm{which}", m - 1))], aggr)

    def root(which, m):
        c = pool.step(f"eps{which}", [ev[(f"aggr{which}", m)], get((f"norm{which}", m - 1))],
                      lambda: G.tensor_scalar(rstd[:, which, :], mv[:, which, :, 1], EPS, None, ALU.add))
        ev[(f"rstd{which}", m)] = pool.step(f"rstd{which}", [c, half_set],
                      lambda: G.tensor_tensor(rstd[:, which, :], rstd[:, which, :], minus_half[:, :], ALU.pow))

    def normalise(which, m, src_of, dst, dst_free):
        def norm():
            for t in range(NT):
                last = V.tensor_scalar(dst[:, t, :], src_of(t), mv[:, which, t, 0:1], rstd[:, which, t:t + 1],
                                       ALU.subtract, ALU.mult)
            return last
        e = ev[(f"norm{which}", m)] = dve.step(f"norm{which}", [ev[(f"rstd{which}", m)]] + dst_free, norm)
        return e

    def load(m):
        a = sp.dma("x1", [get(("norm0", m - 1)), x1_ready],
                   lambda: nc.sync.dma_start(x1[:, :, :], x1_view[m]))
        if m == 0:
            ev["wdown"] = sp.dma("wdown", [], lambda: nc.sync.dma_start(
                wdown[:, :, :, :], w["wdown"].rearrange("(k p) r q -> p k r q", p=P)))
        moments(0, m, lambda t: x1[:, t, :], [a])

    def norm_in(m):
        normalise(0, m, lambda t: x1[:, t, :], xn, [get(("xT_pe", m - 1))])

    def turn_x(m):
        bank = misc()

        def tr():
            for k in range(KD):
                for t in range(NT):
                    last = T.transpose(bank.t[:, k * C + t * P:k * C + (t + 1) * P], xn[:, t, k * P:(k + 1) * P], ident[:, :])
            return last
        a = ev[("xT_pe", m)] = pe.step("xT", [ev[("norm0", m)], consts] + bank.free, tr)
        b = ev[("xT", m)] = act.step("xT", [a, get(("acc", m - 3))],
                                     lambda: S.copy(xT, bank.t[:, :].rearrange("p (k c) -> p k c", k=KD)))
        bank.free = [b]
        c = act.step("xT_hi", [b, get(("down_pe", m - 3))], lambda: S.copy(xT_hi[:, m % 3, :, :], xT))
        ev[("xT_split", m)] = pool.step("xT_lo", [c], lambda: G.tensor_tensor(
            xT_lo[:, m % 3, :, :], xT, xT_hi[:, m % 3, :, :].bitcast(F32), ALU.subtract))

    def scores(m):
        b = ev[("xT", m)]
        q_done = []
        for half in range(2):
            bank = hbank[half]

            def proj(half=half, bank=bank):
                for j in range(2):
                    for k in range(KD):
                        n = 2 * half + j
                        last = T.matmul(bank.t[:, j * C:(j + 1) * C], wq[:, k, n * P:(n + 1) * P], xT[:, k, :],
                                        start=k == 0, stop=k == KD - 1)
                return last
            c = pe.step("q", [b, wq_in] + bank.free, proj)

            def evac(half=half, bank=bank):
                for j in range(2):
                    n = 2 * half + j
                    last = S.activation(qT[:, n, :], bank.t[:, j * C:(j + 1) * C], ACT.Identity, bias=bq[:, n:n + 1])
                return last
            d = act.step("q", [c, consts, get(("score_pe", m - 1)), get(("acc", m - 3))], evac)
            bank.free = [d]
            q_done.append(d)
        for half in range(2):
            for t in range(NT):
                bank = (hbank if half else mbank)[t]

                def sc(t=t, half=half, bank=bank):
                    for j in range(2):
                        last = T.matmul(bank.t[:, j * 256:(j + 1) * 256], qT[:, 2 * half + j, t * P:(t + 1) * P], keys[:, :],
                                        start=True, stop=True)
                    return last
                e = pe.step("score", [q_done[half], consts] + bank.free, sc)
                f = act.step("score", [e, get(("picks_pe", m - 1))],
                             lambda t=t, half=half, bank=bank: S.copy(
                                 score[:, t, 8 * half:8 * half + 8, :].rearrange("p l n -> p (l n)"), bank.t[:, :]))
                bank.free = [f]
                ev[("score", m, t)] = f
        ev[("score_pe", m)] = e

    def top_ten(name, lists, src, vals, ids, ready):
        def each(f):
            def run():
                for l in range(lists):
                    last = f(l)
                return last
            return run
        a = dve.step(name, ready, each(lambda l: V.max(vals(l)[:, 0:8], src(l))))
        b = dve.step(name, [a], each(lambda l: V.max_index(ids(l)[:, 0:8], vals(l)[:, 0:8], src(l))))
        c = dve.step(name, [b], each(lambda l: V.match_replace(src(l), vals(l)[:, 0:8], src(l), GONE)))
        d = dve.step(name, [c], each(lambda l: V.max(vals(l)[:, 8:16], src(l))))
        return dve.step(name, [d], each(lambda l: V.max_index(ids(l)[:, 8:16], vals(l)[:, 8:16], src(l))))

    def lists_top(m, t):
        ev[("lists", m, t)] = top_ten(f"lists{t}", LISTS, lambda l: score[:, t, l, :], lambda l: val[:, t, l, :],
                                      lambda l: idx[:, t, l, :],
                                      [ev[("score", m, t)], get(("cand", m - 1, t)), get(("ids_f", m - 1, t))])

    def numbers(m, t):
        i = idx[:, t, :, :].rearrange("p (h s) k -> p h s k", s=2)

        def ids_f():
            V.tensor_scalar(id1[:, t, :, :], i[:, :, 0, 0:TOPK], float(NSQ), -2048.0, ALU.mult, ALU.add)
            return V.tensor_scalar(id2[:, t, :, :], i[:, :, 1, 0:TOPK], 0.0, None, ALU.add)
        ev[("ids_f", m, t)] = dve.step("ids_f", [ev[("lists", m, t)], get(("cid", m - 1, t))], ids_f)

    pairing = [(pool, G)] + [(dve, V)] * (NT - 1)

    def pairs_of(eng, dst, one, two):
        for a0, na, nb, off in PAIRS:
            last = eng.tensor_tensor(dst[:, :, off:off + na * nb].rearrange("p h (a b) -> p h a b", a=na),
                                   one[:, :, a0:a0 + na].unsqueeze(3).to_broadcast([P, HEADS, na, nb]),
                                   two[:, :, 0:nb].unsqueeze(2).to_broadcast([P, HEADS, na, nb]), ALU.add)
        return last

    def pair_sums(m, t):
        v = val[:, t, :, :].rearrange("p (h s) k -> p h s k", s=2)
        queue, engine = pairing[t]
        ev[("cand", m, t)] = queue.step("cand", [ev[("lists", m, t)], get(("pairs", m - 1, t))], lambda: pairs_of(
            engine, cand[:, t, :, :], v[:, :, 0, :], v[:, :, 1, :]))

    def pair_numbers(m, t):
        queue, engine = pairing[t]
        ev[("cid", m, t)] = queue.step("cid", [ev[("ids_f", m, t)], get(("picks", m - 1))], lambda: pairs_of(
            engine, cid[:, :, :, t], id1[:, t, :, :], id2[:, t, :, :]))

    def pairs_top(m, t):
        ev[("pairs", m, t)] = top_ten(f"pairs{t}", HEADS, lambda l: cand[:, t, l, :], lambda l: top[:, t * HEADS + l, :],
                                      lambda l: pos[:, t * HEADS + l, :],
                                      [ev[("cand", m, t)], get(("shift", m - 1)), get(("posf", m - 1))])

    def pick(m):
        def make_posf():
            for t in range(NT):
                last = V.tensor_copy(posf[:, :, t].rearrange("p (h k) -> p h k", h=HEADS),
                                     pos[:, t * HEADS:(t + 1) * HEADS, 0:TOPK])
            return last
        j = ev[("posf", m)] = dve.step("posf", [ev[("pairs", m, NT - 1)], get(("picks", m - 1))], make_posf)
        k = dve.step("mask", [j, consts, get(("picks_pe", m - 1))], lambda: V.tensor_tensor(
            work[:, :].rearrange("p (s c t) -> p s c t", s=SLOTS, c=NPAIR),
            posf[:, :, :].unsqueeze(2).to_broadcast([P, SLOTS, NPAIR, NT]),
            pair_no[:, :].rearrange("p (c t) -> p c t", t=NT).unsqueeze(1).to_broadcast([P, SLOTS, NPAIR, NT]), ALU.is_equal))
        w4 = work[:, :].rearrange("p (h k c) -> p h k c", h=HEADS, k=TOPK)
        ev[("picks", m)] = dve.step("picks", [k] + [ev[("cid", m, t)] for t in range(NT)], lambda: V.tensor_tensor(
            w4, w4, cid[:, :, :, :].rearrange("p h c t -> p h (c t)").unsqueeze(2).to_broadcast([P, HEADS, TOPK, NPAIR * NT]),
            ALU.mult))

    def pick_gates(m):
        TH = NT * HEADS
        g4 = gate[:, :, :].rearrange("p t (h k) -> p (t h) k", k=TOPK)
        e = ev[("shift", m)] = pool.step("shift", [ev[("pairs", m, NT - 1)], get(("gate_pe", m - 1))], lambda: G.tensor_tensor(
            g4, top[:, :, 0:TOPK], top[:, :, 0:1].to_broadcast([P, TH, TOPK]), ALU.subtract))
        f = act.step("exp", [e], lambda: S.activation(g4, g4, ACT.Exp))
        g = dve.step("gsum", [f], lambda: V.tensor_reduce(gsum[:, :], g4, AX.X, ALU.add))
        h = dve.step("grecip", [g], lambda: V.reciprocal(gsum[:, :], gsum[:, :]))
        ev[("gate", m)] = pool.step("gate", [h], lambda: G.tensor_tensor(
            g4, g4, gsum[:, :].unsqueeze(2).to_broadcast([P, TH, TOPK]), ALU.mult))

    def turn_picks(m):
        bank = misc()
        pk = work[:, :].rearrange("p (s c t) -> p s c t", s=SLOTS, c=NPAIR)
        rows = bank.t[:, 0:NT * SLOTS].rearrange("p (s t) -> p s t", t=NT)

        def over_pairs():
            for c in range(NPAIR):
                last = T.matmul(rows, ident16[:, :], pk[:, :, c, :], start=c == 0, stop=c == NPAIR - 1)
            return last
        a = ev[("picks_pe", m)] = pe.step("picks", [ev[("picks", m)], consts] + bank.free, over_pairs)
        b = act.step("picked", [a, get(("picked_pe", m - 1))], lambda: S.copy(
            picked[:, :, :].rearrange("p t s -> p s t"), rows))
        bank.free = [b]
        bank = misc()

        def turn():
            for t in range(NT):
                last = T.matmul(bank.t[0:SLOTS, t * P:(t + 1) * P], picked[:, t, :], ident16[:, :], start=True, stop=True)
            return last
        a = ev[("picked_pe", m)] = pe.step("picked", [b] + bank.free, turn)
        b = dve.step("eid", [a], lambda: V.tensor_scalar(eid[:, 0, :], bank.t[0:SLOTS, 0:C], 2048.0, None, ALU.add))
        bank.free = [b]

        def fields():
            V.tensor_scalar(eid[:, 1, :], eid[:, 0, :], 6, None, ALU.logical_shift_right)
            V.tensor_scalar(eid[:, 2, :], eid[:, 0, :], 1, None, ALU.bitwise_and)
            return V.tensor_scalar(eid[:, 3, :], eid[:, 0, :], 1, NR - 1, ALU.logical_shift_right, ALU.bitwise_and)
        c = dve.step("fields", [b], fields)
        ev[("qid", m)] = dve.step("qid", [c, get(("ohq", m - 1)), get(("qid_act", m - 1))], lambda: V.scalar_tensor_tensor(
            qid[:, :], eid[:, 2, :], float(NSQ), eid[:, 1, :], ALU.mult, ALU.add))
        ev[("fields", m)] = c

    def turn_r(m):
        ev[("rid", m)] = dve.step("rid", [ev[("fields", m)], get(("ohr", m - 2, NT - 1))],
                                  lambda: V.tensor_copy(rid[:, m % 2, :], eid[:, 3, :]))

    def turn_gates(m):
        bank = misc()

        def gates_pe():
            for t in range(NT):
                last = T.transpose(bank.t[0:SLOTS, t * P:(t + 1) * P], gate[:, t, :], ident[:, :])
            return last
        a = ev[("gate_pe", m)] = pe.step("gate", [ev[("gate", m)], consts] + bank.free, gates_pe)
        b = act.step("gateT", [a, get(("gsplit", m - 1))], lambda: S.mul(gateT[:, :], bank.t[0:SLOTS, 0:C], GATE_SCALE))
        bank.free = [b]
        c = act.step("ghi", [b, get(("ohr", m - 2, NT - 1))], lambda: S.copy(ghi[:, m % 2, :], gateT[:, :]))
        act.step("gelu_table", [half_set], lambda: S.activation(unused[:, :], unscale[:, :], ACT.Gelu))
        ev[("gsplit", m)] = dve.step("glo", [c], lambda: V.tensor_tensor(
            glo[:, m % 2, :], gateT[:, :], ghi[:, m % 2, :], ALU.subtract))

    def onehot_r(m, t):
        tok = slice(t * P, (t + 1) * P)
        free = [get(("gates_pe", m, t - 1) if t else ("gates_pe", m - 1, NT - 1))]

        a = dve.step("ohr", [ev[("rid", m)], consts] + free, lambda: V.tensor_tensor(
            ohr[:, 1, :, :].rearrange("p r (n s) -> p r n s", s=2),
            rid[:, m % 2, tok].rearrange("p (n s) -> p n s", s=2).unsqueeze(1).to_broadcast([SLOTS, NR, P // 2, 2]),
            r_no[0:SLOTS, :].rearrange("p (r s) -> p r s", s=2).unsqueeze(2).to_broadcast([SLOTS, NR, P // 2, 2]), ALU.is_equal))
        b = dve.step("ohr_hi", [a, ev[("gsplit", m)]], lambda: V.tensor_tensor(
            ohr[:, 0, :, :], ohr[:, 1, :, :], ghi[:, m % 2, tok].unsqueeze(1).to_broadcast([SLOTS, NR, P]), ALU.mult))
        ev[("ohr", m, t)] = dve.step("ohr_lo", [b], lambda: V.tensor_tensor(
            ohr[:, 1, :, :], ohr[:, 1, :, :], glo[:, m % 2, tok].unsqueeze(1).to_broadcast([SLOTS, NR, P]), ALU.mult))

    def onehot_q(m):
        def hot():
            for q in range(NQ - NQ_ACT):
                last = V.tensor_scalar(ohq[:, q, :], qid[:, :], float(q), 1.0 / GATE_SCALE, ALU.is_equal, ALU.mult)
            return last
        ev[("ohq", m)] = dve.step("ohq", [ev[("qid", m)], get(("gates_pe", m - 1, NT - 1))], hot)

    def onehot_q_act(m, part):
        n = NQ_ACT // NQ_ACT_PARTS
        first = part * n

        def distance():
            for i in range(first, first + n):
                last = S.activation(ohq[:, NQ - NQ_ACT + i, :], qid[:, :], ACT.Abs, bias=minus_q[0:SLOTS, i:i + 1])
            return last
        rows = ohq[:, NQ - NQ_ACT + first:NQ - NQ_ACT + first + n, :]
        a = ev[("qid_act", m)] = act.step("ohq_dist", [ev[("qid", m)], consts, get(("gates_pe", m - 1, NT - 1))], distance)
        ev[("ohq_act", m)] = act.step("ohq", [a, half_set], lambda: S.activation(
            rows, rows, ACT.Relu, bias=unscale[0:SLOTS, :], scale=-1.0 / GATE_SCALE))

    def gate_matrix(m, t):
        for g in range(P // GROUP):
            bank = sbank[g % len(sbank)]

            def mm(g=g, bank=bank):
                for n in range(GROUP):
                    tok = g * GROUP + n
                    for part in range(2):
                        last = T.matmul(bank.t[:, n * NR:(n + 1) * NR], ohq[:, :, t * P + tok], ohr[:, part, :, tok],
                                        start=part == 0, stop=part == 1)
                return last
            a = pe.step("gates", [ev[("ohq", m)], ev[("ohq_act", m)], ev[("ohr", m, t)]] + bank.free, mm)
            tok0 = t * P + g * GROUP
            b = act.step("gates", [a, get(("mix", m - 1))], lambda bank=bank, tok0=tok0: S.copy(
                gates[:, :, tok0:tok0 + GROUP], bank.t[:, :].rearrange("p (n r) -> p r n", r=NR)))
            bank.free = [b]
        ev[("gates_pe", m, t)] = a
        ev[("gates", m)] = b

    def split_down(m, p):
        slot = wd_split[p % WD_SLOTS]
        src = wdown[:, :, 2 * p:2 * p + 2, :]
        free = get(("down", m, p - WD_SLOTS)) if p >= WD_SLOTS else get(("down_pe", m - 1))
        a = act.step("wd_hi", [ev["wdown"], free], lambda: S.copy(slot[:, 0, :, :, :], src))
        ev[("wd_split", m, p)] = pool.step("wd_lo", [a], lambda: G.tensor_tensor(
            slot[:, 1, :, :, :], src, slot[:, 0, :, :, :].bitcast(F32), ALU.subtract))

    def experts(m, between):
        mixed, wup_in = {}, {}
        for p in range(NR // 2 + LAG):
            for work_of_next in between.get(p, []):
                work_of_next()
            if p < NR // 2:
                bank, slot = hbank[p % 2], p % 4
                n = m * (NR // 2) + p

                def down(p=p, bank=bank):
                    wd = wd_split[p % WD_SLOTS]
                    for j in range(2):
                        parts = [(wd[:, w_part, k, j, :], x_part[:, m % 3, k, :]) for k in range(KD)
                                 for w_part, x_part in ((0, xT_hi), (0, xT_lo), (1, xT_hi))]
                        for i, (a, c) in enumerate(parts):
                            last = T.matmul(bank.t[:, j * C:(j + 1) * C], a, c, start=i == 0, stop=i == len(parts) - 1)
                    return last
                a = ev[("down", m, p)] = pe.step("down", [ev[("xT_split", m)], ev[("wd_split", m, p)]] + bank.free, down)
                if p + WD_SLOTS < NR // 2:
                    split_down(m, p + WD_SLOTS)
                scored = get(("score_pe", m + 2)) if p < 4 else None
                split = get(("xT_split", m + 2)) if p == 3 else None
                b = act.step("gelu", [a, get(("up", n - 4)), scored, split], lambda bank=bank, slot=slot: S.activation(
                    hid[:, slot, :, :], bank.t[:, :].rearrange("p (j c) -> p j c", j=2), ACT.Gelu))
                bank.free = [b]
                mixed[p] = ev[("mix", m)] = pool.step("mix", [b, ev[("gates", m)]], lambda p=p, slot=slot: G.tensor_tensor(
                    hid[:, slot, :, :], hid[:, slot, :, :], gates[:, 2 * p:2 * p + 2, :], ALU.mult))
                wup_in[p] = sp.dma(f"wup{slot}", [get(("up", n - 4))], lambda p=p, slot=slot: nc.sync.dma_start(
                    wup[:, slot, :, :], w["wup"][:, 2 * p:2 * p + 2, :]))
            if p >= LAG:
                u = p - LAG

                def up(u=u):
                    for j in range(2):
                        for t in range(NT):
                            last = T.matmul(abank.t[:, t * D:(t + 1) * D], hid[:, u % 4, j, t * P:(t + 1) * P],
                                            wup[:, u % 4, j, :], start=u == 0 and j == 0 and t == 0,
                                            stop=u == NR // 2 - 1 and j == 1 and t == NT - 1, skip_group_check=True)
                    return last
                free = abank.free if u == 0 else []
                ev[("up", m * (NR // 2) + u)] = pe.step("up", [mixed[u], wup_in[u]] + free, up)
        ev[("down_pe", m)] = a
        ev[("acc", m)] = ev[("up", m * (NR // 2) + NR // 2 - 1)]

    def finish(m):
        moments(1, m, lambda t: abank.t[:, t * D:(t + 1) * D], [ev[("acc", m)]])

    def store(m):
        a = sp.dma("x1t", [get(("res", m - 1)), x1_ready],
                   lambda: nc.sync.dma_start(x1t[:, :, :], x1_view[m]))
        e = normalise(1, m, lambda t: abank.t[:, t * D:(t + 1) * D], y, [get(("out", m - 1))])
        abank.free = [e]
        r = ev[("res", m)] = pool.step("res", [a, e], lambda: G.tensor_tensor(y[:, :, :], y[:, :, :], x1t[:, :, :], ALU.add))
        ev[("out", m)] = sp.dma("out", [r], lambda: nc.sync.dma_start(out_view[m], y[:, :, :]))

    def has(m):
        return 0 <= m < chunks

    for m in range(-3, chunks + 1):
        one, two, three = has(m + 1), has(m + 2), has(m + 3)
        if has(m):
            gate_matrix(m, 0)
            onehot_r(m, 1)
        if two:
            turn_x(m + 2)
        if one:
            turn_picks(m + 1)
            turn_r(m + 1)
        if has(m - 1):
            finish(m - 1)
            root(1, m - 1)
        if one:
            turn_gates(m + 1)
        if has(m - 1):
            store(m - 1)
        if two:
            scores(m + 2)
            lists_top(m + 2, 0)
            numbers(m + 2, 0)
        if has(m):
            gate_matrix(m, 1)
        if three:
            load(m + 3)
        if one:
            onehot_q(m + 1)
            onehot_r(m + 1, 0)
        if two:
            lists_top(m + 2, 1)
            numbers(m + 2, 1)
        between = {p: [] for p in range(NR // 2 + LAG)}
        if one:
            for part in range(NQ_ACT_PARTS):
                between[4 + 2 * part].append(lambda part=part: onehot_q_act(m + 1, part))
        if two:
            between[4].append(lambda: pair_sums(m + 2, 0))
            between[5].append(lambda: pair_numbers(m + 2, 0))
        if two:
            between[NR // 2].append(lambda: pick_gates(m + 2))
        if one:
            between[NR // 2] += [lambda p=p: split_down(m + 1, p) for p in range(WD_SLOTS)]
        if three:
            between[7].append(lambda: root(0, m + 3))
        if two:
            between[14] += [lambda: pair_sums(m + 2, 1), lambda: pair_numbers(m + 2, 1), lambda: pairs_top(m + 2, 0),
                            lambda: pairs_top(m + 2, 1), lambda: pick(m + 2)]
        if three:
            between[14].append(lambda: norm_in(m + 3))
        if has(m):
            experts(m, between)
        else:
            for fs in between.values():
                for f in fs:
                    f()
    sp.last_wait([ev[("out", chunks - 1)]])
    return pe, act, dve, pool, sp


CA = 512
TA = CA // P
MAGIC = 12582912.0
TWO_PI = (6.28125, 0.0019350051879882812, 3.0199159819567534e-07)
PI = 3.1415925


def attention_phase(nc, ctx, sems, seqs, length, x_dram, x1_dram, w):
    sb = lambda name, shape, dt=F32: ctx.enter_context(nc.sbuf_tensor(name, shape, dt))
    ps = lambda name: Bank(ctx.enter_context(nc.psum_tensor(name, [P, 512], F32)))
    pe, act, dve, pool, sp = (Queue(nc, sems, t) for t in ("pe_a", "act_a", "dve_a", "pool_a", "sp_a"))
    T, V, S, G = nc.tensor, nc.vector, nc.scalar, nc.gpsimd
    chunks = seqs * length // CA

    ident, tri, last_row, ones = (sb(f"a_{n}", [P, P]) for n in ("ident", "tri", "last_row", "ones"))
    wproj = sb("a_wproj", [P, 2, KD, 3 * D], F32R)
    wg1 = sb("a_wg1", [P, 2, 2 * KD, D], F32R)
    wb1 = sb("a_wb1", [P, 2, KD, P], F32R)
    zeros = sb("a_zeros", [P, KD])
    wo = sb("a_wo", [P, KD, D])
    wg2 = sb("a_wg2", [P, KD])
    wb2 = sb("a_wb2", [P, 2])
    cols = sb("a_cols", [P, 7])
    head_b = sb("a_head_b", [P, 3])
    bsplit = sb("a_bsplit", [3, 5 * D], BF16)
    row_mask = sb("a_row_mask", [3, 3])
    ones3 = sb("a_ones3", [3, P], BF16)
    minus_half = sb("a_minus_half", [P, TA])
    half_pi = sb("a_half_pi", [P, 1])
    ph = sb("a_ph", [P, TA * D])
    turns = sb("a_turns", [P, TA * D])
    cs = sb("a_cs", [P, 2, TA, 2, D])
    x = sb("a_x", [P, 4, TA, D])
    xn = sb("a_xn", [P, 4, TA, D])
    xT = sb("a_xT", [P, 4, 2, KD, CA + 1], F32R)
    th = sb("a_th", [P, TA, D])
    tha = sb("a_tha", [P, TA, D])
    key = sb("a_key", [P, 2, TA, 2, D])
    keysh = sb("a_keysh", [P, 2, TA, 2, D])
    gh = sb("a_gh", [P, 3, CA])
    z = sb("a_z", [P, TA, 3])
    zmax = sb("a_zmax", [P, TA])
    den = sb("a_den", [P, 2, TA])
    gates = sb("a_gates", [P, 2, TA])
    gcum = sb("a_gcum", [P, 4, TA])
    fac = sb("a_fac", [P, 2, 2, TA])
    u = sb("a_u", [P, 2, 4 * D])
    carry = sb("a_carry", [P, seqs, 4 * D])
    prod = sb("a_prod", [P, 2, 2, 2, D])
    flat = cs[0:3, :, :, :, :].rearrange("p a t s d -> p (a t s d)")
    brow, brest, bsum = (flat[:, i * 5 * D:(i + 1) * 5 * D] for i in range(3))
    bpart = prod[0:3, :, :, :, :].rearrange("p a b c d -> p (a b c d)")[:, 0:3 * 5 * D // 2].bitcast(BF16).rearrange(
        "p (i n) -> p i n", i=3)
    flat = key[:, :, :, :, :].rearrange("p a t s d -> p (a t s d)")
    ends = [0, KD * 3 * D, KD * 5 * D, KD * 5 * D + KD * P]
    whole_proj, whole_g1, whole_b1 = (flat[:, i:j].rearrange("p (k n) -> p k n", k=k)
                                      for i, j, k in zip(ends, ends[1:], (KD, 2 * KD, KD)))
    ret = sb("a_ret", [P, 2, 2, D])
    bl = sb("a_bl", [P, 2, TA, D])
    lnT = sb("a_lnT", [P, KD, CA])
    y = sb("a_y", [P, TA, D])
    stat = sb("a_stat", [P, 3, TA, 6])
    mv = sb("a_mv", [P, 3, TA, 2])
    rstd = sb("a_rstd", [P, 3, TA])
    tbank = [ps("a_ps_t0"), ps("a_ps_t1")]
    fbank = [ps("a_ps_f0"), ps("a_ps_f1")]
    pbank = [ps("a_ps_p0"), ps("a_ps_p1")]
    cbank = [ps("a_ps_c0"), ps("a_ps_c1")]
    turn_of = {"t": 0, "f": 0, "p": 0}

    def bank_of(kind):
        turn_of[kind] += 1
        return {"t": tbank, "f": fbank, "p": pbank}[kind][turn_of[kind] % 2]

    ev = {}
    get = ev.get

    def three(w_parts, x_parts):
        return [(w_parts(i), x_parts(j)) for i, j in ((0, 0), (0, 1), (1, 0))]

    def where(n):
        j, b = divmod(n, seqs)
        rows = slice(b * length + j * CA, b * length + (j + 1) * CA)
        return j, b, rows

    def rows_of(dram, rows):
        return dram[rows, :].rearrange("(t p) d -> p t d", p=P)

    def load(n):
        j, b, rows = where(n)
        if ("x", n) not in ev:
            ev[("x", n)] = sp.dma(f"x{n % 4}", [get(("x1", n - 4))],
                                  lambda: nc.sync.dma_start(x[:, n % 4, :, :], rows_of(x_dram, rows)))

    load(0)
    loaded = None
    by_k = lambda a: a.rearrange("(k p) n -> p k n", p=P)
    for dst, src in ((ident[:, :], w["ident"]), (tri[:, :], w["tri"]), (last_row[:, :], w["last_row"]), (ones[:, :], w["ones"]),
                     (whole_proj[:, :, 0:D], by_k(w["wpv"])), (whole_proj[:, :, D:2 * D], by_k(w["wkv"])),
                     (whole_proj[:, :, 2 * D:3 * D], by_k(w["wk"])), (whole_g1, by_k(w["wg1"])), (whole_b1, by_k(w["wb1"])),
                     (wo[:, :, :], by_k(w["wo"])), (wg2[:, :], w["wg2"]), (wb2[:, :], w["wb2"]), (cols[:, :], w["cols"]),
                     (head_b[:, :], w["head_b"]), (brow, w["brow"]), (row_mask[:, :], w["row_mask"])):
        loaded = sp.dma("weights", [], lambda dst=dst, src=src: nc.sync.dma_start(dst, src))

    def set_constants():
        G.memset(minus_half[:, :], -0.5)
        G.memset(half_pi[:, :], PI / 2)
        G.memset(ones3[:, :], 1.0)
        for b in range(seqs):
            G.memset(keysh[0:1, b, 0, :, :], 0.0)
        G.memset(zeros[:, :], 0.0)
        return G.memset(carry[:, :, :], 0.0)
    constants = pool.step("constants", [], set_constants)

    pairs = ((wproj, whole_proj), (wg1, whole_g1), (wb1, whole_b1))

    def high_parts():
        for parts, whole in pairs:
            last = S.copy(parts[:, 0, :, :], whole)
        return last

    def low_parts():
        for parts, whole in pairs:
            last = V.tensor_tensor(parts[:, 1, :, :], whole, parts[:, 0, :, :].bitcast(F32), ALU.subtract)
        return last
    s = act.step("w_high", [loaded], high_parts)
    split = dve.step("w_low", [s], low_parts)

    s = dve.step("bias0", [loaded], lambda: V.tensor_copy(bpart[:, 0, :], brow))
    s = dve.step("bias1", [s], lambda: V.tensor_tensor(brest, brow, bpart[:, 0, :], ALU.subtract))
    s = dve.step("bias2", [s], lambda: V.tensor_copy(bpart[:, 1, :], brest))
    s = dve.step("bias3", [s], lambda: V.tensor_tensor(brest, brest, bpart[:, 1, :], ALU.subtract))
    s = dve.step("bias4", [s], lambda: V.tensor_copy(bpart[:, 2, :], brest))
    s = dve.step("bias5", [s], lambda: V.tensor_scalar(bsum, bpart[:, 0, :], row_mask[:, 0:1], None, ALU.mult))
    s = dve.step("bias6", [s], lambda: V.scalar_tensor_tensor(bsum, bpart[:, 1, :], row_mask[:, 1:2], bsum,
                                                              ALU.mult, ALU.add))
    bias = dve.step("bias7", [s], lambda: V.scalar_tensor_tensor(bsplit[:, :], bpart[:, 2, :], row_mask[:, 2:3], bsum,
                                                                 ALU.mult, ALU.add))

    def moments(which, n, src, ready):
        def stats():
            for t in range(TA):
                last = V.bn_stats(stat[:, which, t, :], src(t))
            return last
        a = dve.step(f"stats{which}", ready + [get((f"aggr{which}", n - 1))], stats)

        def aggr():
            for t in range(TA):
                last = V.bn_aggr(mv[:, which, t, :], stat[:, which, t, :])
            return last
        b = ev[(f"aggr{which}", n)] = dve.step(f"aggr{which}", [a, get((f"norm{which}", n - 1))], aggr)
        c = pool.step(f"eps{which}", [b, get((f"norm{which}", n - 1))],
                      lambda: G.tensor_scalar(rstd[:, which, :], mv[:, which, :, 1], EPS, None, ALU.add))
        ev[(f"rstd{which}", n)] = pool.step(f"rstd{which}", [c, constants],
                      lambda: G.tensor_tensor(rstd[:, which, :], rstd[:, which, :], minus_half[:, :], ALU.pow))

    def normalise(which, n, src, dst, dst_free):
        def norm():
            for t in range(TA):
                last = V.tensor_scalar(dst(t), src(t), mv[:, which, t, 0:1], rstd[:, which, t:t + 1], ALU.subtract, ALU.mult)
            return last
        e = ev[(f"norm{which}", n)] = dve.step(f"norm{which}", [ev[(f"rstd{which}", n)]] + dst_free, norm)
        return e

    def moments_in(n):
        moments(0, n, lambda t: x[:, n % 4, t, :], [ev[("x", n)]])

    def norm_in(n):
        normalise(0, n, lambda t: x[:, n % 4, t, :], lambda t: xn[:, n % 4, t, :], [get(("y", n - 4))])

    def load_phases(n):
        j = n // seqs
        if n % seqs == 0:
            ev[("ph", j)] = sp.dma("ph", [get(("cs", j - 1))], lambda: nc.sync.dma_start(
                ph[:, :].rearrange("p (t d) -> p t d", t=TA), rows_of(w["phases"], slice(j * CA, (j + 1) * CA))))

    def reduce_phases(n):
        j = n // seqs
        if n % seqs:
            return
        b = dve.step("turns", [ev[("ph", j)], get(("cs", j - 1))], lambda: V.tensor_scalar(
            turns[:, :], ph[:, :], 0.15915494309189535, MAGIC, ALU.mult, ALU.add))
        b = dve.step("turns", [b], lambda: V.tensor_scalar(turns[:, :], turns[:, :], MAGIC, None, ALU.subtract))
        for part in TWO_PI:
            b = dve.step("reduce", [b], lambda part=part: V.scalar_tensor_tensor(
                ph[:, :], turns[:, :], -part, ph[:, :], ALU.mult, ALU.add))
        ev[("reduced", j)] = dve.step("clamp", [b], lambda: V.tensor_scalar(ph[:, :], ph[:, :], -PI, PI, ALU.max, ALU.min))

    def waves(n):
        j, slot = n // seqs, n // seqs % 2
        if n % seqs:
            return
        c = act.step("ph_abs", [ev[("reduced", j)]], lambda: S.activation(turns[:, :], ph[:, :], ACT.Abs))
        four = lambda a: a.rearrange("p (t d) -> p t d", t=TA)

        def both():
            S.activation(cs[:, slot, :, 1, :], four(ph[:, :]), ACT.Sin)
            return S.activation(cs[:, slot, :, 0, :], four(turns[:, :]), ACT.Sin, bias=half_pi[:, :], scale=-1.0)
        ev[("cs", j)] = act.step("cs", [c, constants, bias, get(("prod", (j - 2) * seqs + seqs - 1, TA - 1))], both)

    def turn_x(n):
        j, b, _ = where(n)
        slot = n % 4
        done = []
        for k in range(KD):
            bank = bank_of("t")

            def tr(k=k, bank=bank):
                for t in range(TA):
                    last = T.transpose(bank.t[:, t * P:(t + 1) * P], xn[:, slot, t, k * P:(k + 1) * P], ident[:, :])
                return last
            a = pe.step("xT", [ev[("norm0", n)], loaded] + bank.free, tr)
            c = act.step("xT", [a, get(("pv_pe", n - 4))], lambda k=k, bank=bank: S.copy(
                xT[:, slot, 0, k, 1:CA + 1], bank.t[:, :]))
            c = dve.step("xT_lo", [c], lambda k=k, bank=bank: V.tensor_tensor(
                xT[:, slot, 1, k, 1:CA + 1], bank.t[:, :], xT[:, slot, 0, k, 1:CA + 1].bitcast(F32), ALU.subtract))
            bank.free = [c]
        def before():
            for part in range(2):
                src = xT[:, (n - seqs) % 4, part, :, CA:CA + 1].bitcast(F32) if j else zeros[:, :].unsqueeze(2)
                last = S.copy(xT[:, slot, part, :, 0:1], src)
            return last
        d = act.step("x_before", [c, constants, get(("xT", n - seqs))], before)
        ev[("xT", n)] = c
        ev[("x_before", n)] = d

    def keys(n):
        j, b, _ = where(n)
        slot = n % 2
        for half in range(2):
            bank = bank_of("f")

            def proj(half=half, bank=bank):
                T.matmul(bank.t[:, 0:D], ones3[:, :], bsplit[:, 2 * D:3 * D], start=True, stop=False, skip_group_check=True)
                T.matmul(bank.t[:, D:2 * D], ones3[:, :], bsplit[:, 2 * D:3 * D], start=False, stop=False, skip_group_check=True)
                for i in range(2):
                    t = 2 * half + i
                    for k in range(KD):
                        for part, (wp, xp) in enumerate(three(lambda p: wproj[:, p, k, 2 * D:3 * D],
                                                              lambda p: xT[:, n % 4, p, k, 1 + t * P:1 + (t + 1) * P])):
                            last = T.matmul(bank.t[:, i * D:(i + 1) * D], xp, wp, start=False,
                                            stop=i == 1 and k == KD - 1 and part == 2, skip_group_check=True)
                return last
            a = pe.step("keys", [ev[("xT", n)], split, bias, constants] + bank.free, proj)
            c = act.step("tanh", [a, get(("key", n - 1))], lambda half=half, bank=bank: S.activation(
                th[:, 2 * half:2 * half + 2, :], bank.t[:, :].rearrange("p (t d) -> p t d", t=2), ACT.Tanh))
            bank.free = [c]
        ev[("tanh", n)] = c

    def key_waves(n):
        j, b, _ = where(n)
        slot = n % 2
        d = act.step("th_abs", [ev[("tanh", n)]], lambda: S.activation(tha[:, :, :], th[:, :, :], ACT.Abs))

        def both():
            S.activation(key[:, slot, :, 1, :], th[:, :, :], ACT.Sin, scale=PI)
            return S.activation(key[:, slot, :, 0, :], tha[:, :, :], ACT.Sin, bias=half_pi[:, :], scale=-PI)
        e = ev[("key", n)] = act.step("key", [
            d, constants, split, get(("prod", n - 2, TA - 1)), get(("keysh_in", n - 2)), get(("key_end", n - 2))], both)
        free = get(("u", n - 2, TA - 1))
        moves = [(keysh[1:113, slot, :, :, :], key[0:112, slot, :, :, :]),
                 (keysh[113:128, slot, :, :, :], key[112:127, slot, :, :, :]),
                 (keysh[0:1, slot, 1:TA, :, :], key[127:128, slot, 0:TA - 1, :, :])]
        for dst, src in moves:
            f = sp.dma(f"keysh{slot}", [e, free], lambda dst=dst, src=src: nc.sync.dma_start(dst, src))
        if j:
            f = sp.dma(f"keysh{slot}", [free, ev[("key_end", n - seqs)]],
                       lambda: nc.sync.dma_start(keysh[0:1, slot, 0, :, :], key_end[0:1, b, :, :]))
        ev[("key_end", n)] = sp.dma(f"key_end{b}", [e, f],
                                        lambda: nc.sync.dma_start(key_end[0:1, b, :, :], key[127:128, slot, TA - 1, :, :]))
        ev[("keysh_in", n)] = f

    key_end = sb("a_key_end", [1, seqs, 2, D])

    def gating(n):
        j, b, _ = where(n)
        slot = n % 4
        for m in range(3):
            bank = bank_of("f")

            def hidden(m=m, bank=bank):
                tok = lambda first, k: lambda p: xT[:, slot, p, k, first:first + CA]
                parts = []
                for k in range(KD):
                    if m < 2:
                        parts += three(lambda p: wg1[:, p, k, m * P:(m + 1) * P], tok(1, k))
                        parts += three(lambda p: wg1[:, p, KD + k, m * P:(m + 1) * P], tok(0, k))
                    else:
                        parts += three(lambda p: wb1[:, p, k, :], tok(1, k))
                for i, (a, c) in enumerate(parts):
                    last = T.matmul(bank.t[:, :], a, c, start=i == 0, stop=i == len(parts) - 1)
                return last
            a = pe.step("hidden", [ev[("xT", n)], ev[("x_before", n)], split] + bank.free, hidden)
            c = act.step("hidden", [a, get(("logits", n - 1))], lambda m=m, bank=bank: S.activation(
                gh[:, m, :], bank.t[:, :], ACT.Gelu, bias=cols[:, m:m + 1]))
            bank.free = [c]
        ev[("hidden", n)] = c

    def gate_values(n):
        bank = bank_of("f")

        def logits():
            for t in range(TA):
                tok = slice(t * P, (t + 1) * P)
                for m in range(2):
                    T.matmul(bank.t[:, 3 * t:3 * t + 1], gh[:, m, tok], wg2[:, m:m + 1], start=m == 0, stop=m == 1)
                last = T.matmul(bank.t[:, 3 * t + 1:3 * t + 3], gh[:, 2, tok], wb2[:, :], start=True, stop=True)
            return last
        a = ev[("logits", n)] = pe.step("logits", [ev[("hidden", n)]] + bank.free, logits)
        s = dve.step("z", [a, get(("fac", n - 1))], lambda: V.tensor_tensor(
            z[:, :, :], bank.t[:, 0:3 * TA].rearrange("p (t c) -> p t c", c=3),
            head_b[:, :].unsqueeze(1).to_broadcast([P, TA, 3]), ALU.add))
        bank.free = [s]
        s = dve.step("zmax", [s], lambda: V.tensor_tensor(zmax[:, :], z[:, :, 1], z[:, :, 2], ALU.max))

        def shift():
            V.tensor_scalar(z[:, :, 0], z[:, :, 0], -1.0, None, ALU.mult)
            return V.tensor_tensor(z[:, :, 1:3], z[:, :, 1:3], zmax[:, :].unsqueeze(2).to_broadcast([P, TA, 2]), ALU.subtract)
        s = dve.step("zshift", [s], shift)
        s = act.step("exp", [s], lambda: S.activation(z[:, :, :], z[:, :, :], ACT.Exp))

        def sums():
            V.tensor_scalar(den[:, 0, :], z[:, :, 0], 1.0, None, ALU.add)
            return V.tensor_tensor(den[:, 1, :], z[:, :, 1], z[:, :, 2], ALU.add)
        s = dve.step("den", [s], sums)
        s = dve.step("recip", [s], lambda: V.reciprocal(den[:, :, :], den[:, :, :]))

        s = dve.step("gate", [s, get(("u", n - 2, TA - 1)), get(("gcum_pe", n - 2))],
                     lambda: V.tensor_copy(gates[:, n % 2, :], den[:, 0, :]))
        ev[("gate", n)] = s

    def gate_sums(n):
        j, b, _ = where(n)
        gate = ev[("gate", n)]
        bank = bank_of("f")

        def gsum():
            g = gates[:, n % 2, :]
            last = T.matmul(bank.t[:, 0:TA], tri[:, :], g, start=True, stop=False)
            for t in range(TA - 1):
                last = T.matmul(bank.t[:, t + 1:TA], ones[:, :], g[:, t:t + 1].to_broadcast([P, TA - 1 - t]), start=False,
                                stop=not j and t == TA - 2)
            if j:
                last = T.matmul(bank.t[:, 0:TA], last_row[:, :], gcum[:, (n - seqs) % 4, TA - 1:TA].to_broadcast([P, TA]),
                                start=False, stop=True)
            return last
        a = ev[("gcum_pe", n)] = pe.step("gcum", [gate, get(("gcum", n - seqs)) if j else None] + bank.free, gsum)
        s = ev[("gcum", n)] = dve.step("gcum", [a, get(("gcum_pe", n - 2))], lambda: V.tensor_copy(
            gcum[:, n % 4, :], bank.t[:, 0:TA]))
        bank.free = [s]
        s = dve.step("gmax", [s], lambda: V.tensor_scalar(zmax[:, :], gcum[:, n % 4, :], 1.0, None, ALU.max))
        ev[("groot", n)] = pool.step("groot", [s, constants], lambda: G.tensor_tensor(
            zmax[:, :], zmax[:, :], minus_half[:, :], ALU.pow))

    def gate_factors(n):
        s1 = dve.step("zscale", [ev[("groot", n)]], lambda: V.scalar_tensor_tensor(
            z[:, :, 1:3], z[:, :, 1:3], 1.0 / 16, den[:, 1, :].unsqueeze(2).to_broadcast([P, TA, 2]), ALU.mult, ALU.mult))

        def factors():
            V.tensor_copy(fac[:, n % 2, 0, :], z[:, :, 1])
            return V.tensor_tensor(fac[:, n % 2, 1, :], z[:, :, 2], zmax[:, :], ALU.mult)
        ev[("fac", n)] = dve.step("fac", [s1, get(("blend", n - 2, TA - 1))], factors)

    def values(n, t):
        j, b, _ = where(n)
        bank = bank_of("p")

        def proj():
            T.matmul(bank.t[:, :], ones3[:, :], bsplit[:, 0:2 * D], start=True, stop=False)
            for k in range(KD):
                for i, (wp, xp) in enumerate(three(lambda p: wproj[:, p, k, 0:2 * D],
                                                   lambda p: xT[:, n % 4, p, k, 1 + t * P:1 + (t + 1) * P])):
                    last = T.matmul(bank.t[:, :], xp, wp, start=False, stop=k == KD - 1 and i == 2)
            return last
        a = ev[("pv_pe", n)] = pe.step("values", [ev[("xT", n)], split, bias, constants] + bank.free, proj)
        i = (n * TA + t) % 2
        twice = lambda v: v.unsqueeze(1).to_broadcast([P, 2, D])

        def terms():
            V.tensor_tensor(u[:, i, 0:2 * D].rearrange("p (s d) -> p s d", s=2), cs[:, j % 2, t, :, :],
                            twice(bank.t[:, 0:D]), ALU.mult)
            return V.scalar_tensor_tensor(u[:, i, 2 * D:4 * D].rearrange("p (s d) -> p s d", s=2), twice(bank.t[:, D:2 * D]),
                                          gates[:, n % 2, t:t + 1], keysh[:, n % 2, t, :, :], ALU.mult, ALU.mult)
        c = ev[("u", n, t)] = dve.step("u", [a, ev[("cs", j)], ev[("gate", n)], ev[("keysh_in", n)],
                                             get(("sum_pe", n * TA + t - 2))], terms)
        bank.free = [c]

    def sums(n, t):
        j, b, _ = where(n)
        i = (n * TA + t) % 2
        first = j == 0 and t == 0

        def cum():
            for h in range(2):
                last = T.matmul(cbank[h].t[:, :], tri[:, :], u[:, i, h * 512:(h + 1) * 512], start=True, stop=first)
            if not first:
                for h in range(2):
                    last = T.matmul(cbank[h].t[:, :], last_row[:, :], carry[:, b, h * 512:(h + 1) * 512], start=False, stop=True)
            return last
        a = ev[("sum_pe", n * TA + t)] = pe.step("sums", [ev[("u", n, t)], loaded, ev.get(("carry", b)), constants] + cbank[0].free, cum)

        def keep():
            for h in range(2):
                last = S.copy(carry[96:128, b, h * 512:(h + 1) * 512], cbank[h].t[96:128, :])
            return last
        c = ev[("carry", b)] = act.step("carry", [a], keep)

        def back():
            V.tensor_tensor(prod[:, i, 0, :, :], cbank[0].t[:, :].rearrange("p (s d) -> p s d", s=2), cs[:, j % 2, t, :, :], ALU.mult)
            return V.tensor_tensor(prod[:, i, 1, :, :], cbank[1].t[:, :].rearrange("p (s d) -> p s d", s=2),
                                   key[:, n % 2, t, :, :], ALU.mult)
        d = ev[("prod", n, t)] = dve.step("prod", [c, get(("ret", n * TA + t - 2))], back)
        for bank in cbank:
            bank.free = [d]
        e = ev[("ret", n * TA + t)] = pool.step("ret", [d, get(("blend", n * TA + t - 2))], lambda: G.tensor_tensor(
            ret[:, i, :, :], prod[:, i, :, 0, :], prod[:, i, :, 1, :], ALU.add))
        f = pool.step("ret_pos", [e, ev[("fac", n)]], lambda: G.tensor_scalar(
            ret[:, i, 0, :], ret[:, i, 0, :], fac[:, n % 2, 0, t:t + 1], None, ALU.mult))
        ev[("ret_pos", n, t)] = f

    def blend(n, t):
        i = (n * TA + t) % 2
        g = dve.step("blend", [ev[("ret_pos", n, t)], get(("norm1", n - 2))], lambda: V.scalar_tensor_tensor(
            bl[:, n % 2, t, :], ret[:, i, 1, :], fac[:, n % 2, 1, t:t + 1], ret[:, i, 0, :], ALU.mult, ALU.add))
        ev[("blend", n, t)] = ev[("blend", n * TA + t)] = g

    def blend_moments(n):
        moments(1, n, lambda t: bl[:, n % 2, t, :], [ev[("blend", n, TA - 1)]])

    def blend_norm(n):
        normalise(1, n, lambda t: bl[:, n % 2, t, :], lambda t: bl[:, n % 2, t, :], [])

    def turn_blend(n):
        for k in range(KD):
            bank = bank_of("t")

            def tr(k=k, bank=bank):
                for t in range(TA):
                    last = T.transpose(bank.t[:, t * P:(t + 1) * P], bl[:, n % 2, t, k * P:(k + 1) * P], ident[:, :])
                return last
            a = ev[("lnT_pe", n)] = pe.step("lnT", [ev[("norm1", n)]] + bank.free, tr)
            c = act.step("lnT", [a, get(("wo_pe", n - 1)), loaded], lambda k=k, bank=bank: S.activation(
                lnT[:, k, :], bank.t[:, :], ACT.Identity, bias=cols[:, 5 + k:6 + k], scale=cols[:, 3 + k:4 + k]))
            bank.free = [c]
        ev[("lnT", n)] = c

    def project_out(n):
        c = ev[("lnT", n)]
        for half in range(2):
            bank = bank_of("t")

            def proj(half=half, bank=bank):
                T.matmul(bank.t[:, :], ones3[:, :], bsplit[:, 3 * D:5 * D], start=True, stop=False, skip_group_check=True)
                for i in range(2):
                    t = 2 * half + i
                    for k in range(KD):
                        last = T.matmul(bank.t[:, i * D:(i + 1) * D], lnT[:, k, t * P:(t + 1) * P], wo[:, k, :],
                                        start=False, stop=i == 1 and k == KD - 1, skip_group_check=True)
                return last
            a = pe.step("wo", [c, bias] + bank.free, proj)
            d = dve.step("y", [a, get(("x1_out", n - 1))], lambda half=half, bank=bank: V.tensor_tensor(
                y[:, 2 * half:2 * half + 2, :], bank.t[:, :].rearrange("p (t d) -> p t d", t=2),
                xn[:, n % 4, 2 * half:2 * half + 2, :], ALU.add))
            bank.free = [d]
        ev[("wo_pe", n)] = a
        ev[("y", n)] = d
        moments(2, n, lambda t: y[:, t, :], [d])

    def residual(n):
        j, b, rows = where(n)
        e = normalise(2, n, lambda t: y[:, t, :], lambda t: y[:, t, :], [])
        f = ev[("x1", n)] = pool.step("x1", [e, ev[("x", n)]], lambda: G.tensor_tensor(
            y[:, :, :], y[:, :, :], x[:, n % 4, :, :], ALU.add))
        ev[("x1_out", n)] = sp.dma("x1", [f], lambda: nc.sync.dma_start(rows_of(x1_dram, rows), y[:, :, :]))

    for n in range(-2, chunks + 1):
        stages = [(n, values, 0), (n, values, 1), (n + 2, load), (n - 1, blend, TA - 1), (n + 1, turn_x),
                  (n, gate_factors), (n - 1, blend_moments), (n + 2, load_phases), (n, sums, 0), (n + 1, keys),
                  (n + 2, moments_in), (n + 2, reduce_phases), (n - 1, blend_norm), (n, values, 2), (n + 2, norm_in),
                  (n, sums, 1), (n, blend, 0), (n, values, 3), (n + 1, gating), (n, blend, 1), (n + 1, key_waves),
                  (n - 1, turn_blend), (n + 1, gate_values), (n, sums, 2), (n, blend, 2), (n - 1, project_out),
                  (n, sums, 3), (n + 1, waves), (n + 1, gate_sums), (n - 1, residual)]
        for chunk, stage, *tile in stages:
            if 0 <= chunk < chunks:
                stage(chunk, *tile)
    sp.last_wait([ev[("x1_out", chunks - 1)]])
    return (pe, act, dve, pool, sp), ev[("x1_out", chunks - 1)]


def build(nc, x, phases, wpv, wkv, wk, wg1, wg2, wb1, wb2, wo, cols, head_b, brow, row_mask, ident, tri, last_row, ones,
          ident16, wq, bq, keys, wdown, wup, pair_no, r_no, minus_q, out, seqs, length):
    x1 = nc.dram_tensor("x1_between", [seqs * length, D], F32, kind="Internal").ap()
    with ExitStack() as sems:
        with ExitStack() as memory:
            queues, x1_written = attention_phase(
                nc, memory, sems, seqs, length, x, x1,
                dict(phases=phases, wpv=wpv, wkv=wkv, wk=wk, wg1=wg1, wg2=wg2, wb1=wb1, wb2=wb2, wo=wo, cols=cols, head_b=head_b,
                     brow=brow, row_mask=row_mask, ident=ident, tri=tri, last_row=last_row, ones=ones))
            in_blocks(nc, *queues)
        with ExitStack() as memory:
            queues = experts_phase(
                nc, memory, sems, seqs * length // C, x1, out,
                dict(ident=ident, ident16=ident16, pair_no=pair_no, r_no=r_no, minus_q=minus_q, keys=keys,
                     bq=bq, wq=wq, wdown=wdown, wup=wup), x1_written)
            in_blocks(nc, *queues)


def kernel(**inputs):
    import numpy as np
    import concourse.bacc as bacc
    from concourse.bass_utils import run_bass_kernel_spmd

    a = {k.removeprefix("L0_"): np.asarray(v) for k, v in inputs.items()}
    x = a["attn_x"]
    seqs, length, width = x.shape
    by_feature = lambda v: v.reshape(-1, P).T
    in_rows = lambda v, n: np.tile(v, (n, 1))

    def experts_by_qr(table):
        return table[:NSQ * NSQ].reshape(NSQ, NR, 2, width)

    k1, k2 = a["ffn_K1"], a["ffn_K2"]
    half = k1.shape[1]
    keys = np.zeros((P, 4 * NSQ), k1.dtype)
    for i, k in enumerate((k1, k2, k1, k2)):
        keys[i * half:(i + 1) * half, i * NSQ:(i + 1) * NSQ] = k.T
    last_row = np.zeros((P, P), x.dtype)
    last_row[-1] = 1
    arrays = dict(
        x=x.reshape(-1, width), phases=a["attn_pos_phases"][:length],
        wpv=a["attn_Wpv"], wkv=a["attn_Wkv"], wk=a["attn_Wk"], wg1=a["attn_Wg1"], wg2=by_feature(a["attn_Wg2"]),
        wb1=a["attn_Wb1"], wb2=a["attn_Wb2"], wo=a["attn_Wo"],
        cols=np.concatenate([by_feature(a[n]) for n in ("attn_bg1", "attn_bb1", "attn_ln_g", "attn_ln_b")], 1),
        head_b=in_rows(np.concatenate([a["attn_bg2"], a["attn_bb2"]]), P),
        brow=in_rows(np.concatenate([a[n] for n in ("attn_bpv", "attn_bkv", "attn_bk", "attn_bo", "attn_bo")]), 3),
        row_mask=np.eye(3, dtype=x.dtype), ident=np.eye(P, dtype=x.dtype), tri=np.triu(np.ones((P, P), x.dtype)),
        last_row=last_row, ones=np.ones((P, P), x.dtype), ident16=np.eye(P, dtype=np.float16),
        wq=a["ffn_Wq"], bq=by_feature(a["ffn_bq"]), keys=keys,
        wdown=experts_by_qr(a["ffn_W_down"]).transpose(3, 1, 2, 0).reshape(width, NR, NQ),
        wup=experts_by_qr(a["ffn_W_up"]).transpose(2, 0, 1, 3).reshape(NQ, NR, width),
        pair_no=in_rows(np.repeat(np.arange(NPAIR), NT).astype(np.float16), P),
        r_no=in_rows(np.repeat(np.arange(NR), 2).astype(np.float16), P),
        minus_q=in_rows(-np.arange(NQ - NQ_ACT, NQ).astype(x.dtype), P),
    )
    arrays = {k: np.ascontiguousarray(v) for k, v in arrays.items()}
    nc = bacc.Bacc("TRN2", target_bir_lowering=False, num_devices=1,
                   dynamic_dma_scratch_size=1024)
    args = {k: nc.dram_tensor(f"in_{k}", v.shape, mybir.dt.from_np(v.dtype), kind="ExternalInput").ap()
            for k, v in arrays.items()}
    out = nc.dram_tensor("out", [seqs * length, width], F32, kind="ExternalOutput").ap()
    build(nc, out=out, seqs=seqs, length=length, **args)
    got = run_bass_kernel_spmd(nc, [{f"in_{k}": v for k, v in arrays.items()}], core_ids=[0])
    return got.results[0]["out"].reshape(x.shape)
```
